# Optimizing a Trainium2 kernel written in Bass

```python
import numpy as np
import jax
import jax.numpy as jnp

def _softmax(x, axis=-1):
    return jax.nn.softmax(x, axis=axis)

def _gelu(x):
    return jax.nn.gelu(x, approximate=True)

def _silu(x):
    return jax.nn.silu(x)

def _sigmoid(x):
    return jax.nn.sigmoid(x)

def _layernorm(x, axis=-1, eps=1e-05):
    m = jnp.mean(x, axis=axis, keepdims=True)
    v = jnp.var(x, axis=axis, keepdims=True)
    return (x - m) / jnp.sqrt(v + eps)

def _scatter_add(tgt, idx, src, axis=0):
    return tgt.at[idx].add(src)

def _segment_sum(src, seg, n):
    return jax.ops.segment_sum(src, seg, n)
kernel_name = 'mk_seq_preln_d2_jaxref_r8_026ea9'

def setup_inputs(seed: int=0):
    np.random.seed(seed)
    _w = jnp.asarray

    def _L0_attn_setup():
        import jax, jax.numpy as jnp
        import numpy as np
        B, T, D = (4, 256, 128)
        H, Dh = (16, 64)
        key = jax.random.key(seed)
        ks = jax.random.split(key, 5)
        std_qkv = float(np.sqrt(2.0 / (Dh * D)))
        std_o = float(np.sqrt(2.0 / (D * Dh)))
        return {'x': jax.random.normal(ks[0], (B, T, D), dtype=jnp.float32), 'W_Q': jax.random.normal(ks[1], (H, Dh, D), dtype=jnp.float32) * std_qkv, 'b_Q': jnp.zeros((H, Dh), dtype=jnp.float32), 'W_K': jax.random.normal(ks[2], (H, Dh, D), dtype=jnp.float32) * std_qkv, 'b_K': jnp.zeros((H, Dh), dtype=jnp.float32), 'W_V': jax.random.normal(ks[3], (H, Dh, D), dtype=jnp.float32) * std_qkv, 'b_V': jnp.zeros((H, Dh), dtype=jnp.float32), 'W_O': jax.random.normal(ks[4], (H, D, Dh), dtype=jnp.float32) * std_o, 'b_O': jnp.zeros((D,), dtype=jnp.float32)}
    _L0_attn_in = _L0_attn_setup()

    def _L0_ffn_setup():
        import jax, jax.numpy as jnp
        import numpy as np
        NUM_EXPERTS = 8
        IN_FEATURES = 128
        HIDDEN_FEATURES = 512
        GATE_DIM = 16
        EPS = 0.0001
        key = jax.random.key(seed)
        ks = jax.random.split(key, 7)
        hidden_states = jax.random.normal(ks[0], (1, 256, IN_FEATURES), dtype=jnp.float32)
        wg_red = jax.random.normal(ks[1], (GATE_DIM, IN_FEATURES), dtype=jnp.float32) * 0.02
        wg = jax.random.normal(ks[2], (NUM_EXPERTS, GATE_DIM), dtype=jnp.float32)
        w1 = jax.random.uniform(ks[3], (NUM_EXPERTS, IN_FEATURES, HIDDEN_FEATURES), dtype=jnp.float32)
        b1 = jax.random.uniform(ks[4], (NUM_EXPERTS, HIDDEN_FEATURES), dtype=jnp.float32)
        w2 = jax.random.uniform(ks[5], (NUM_EXPERTS, HIDDEN_FEATURES, IN_FEATURES), dtype=jnp.float32)
        b2 = jax.random.uniform(ks[6], (NUM_EXPERTS, IN_FEATURES), dtype=jnp.float32)
        return {'hidden_states': hidden_states, 'wg_red': wg_red, 'wg': wg, 'w1': w1, 'b1': b1, 'w2': w2, 'b2': b2}
    _L0_ffn_in = _L0_ffn_setup()

    def _L1_attn_setup():
        import jax, jax.numpy as jnp
        import numpy as np
        B_SZ, SEQ = (2, 256)
        D_MODEL, D_STATE, D_CONV = (128, 16, 4)
        D_INPUT, D_OUTPUT = (128, 128)
        D_INNER = 2 * D_MODEL
        DT_RANK = D_MODEL // 16
        key = jax.random.key(seed)
        ks = jax.random.split(key, 8)

        def rn(k, shape, scale):
            return (jax.random.normal(k, shape) * scale).astype(jnp.float32)
        return {'x': rn(ks[0], (B_SZ, SEQ, D_INPUT), 1.0), 'fc1_w': rn(ks[1], (D_MODEL, D_INPUT), D_INPUT ** (-0.5)), 'fc1_b': jnp.zeros((D_MODEL,), jnp.float32), 'in_proj_w': rn(ks[2], (2 * D_INNER, D_MODEL), D_MODEL ** (-0.5)), 'conv_w': rn(ks[3], (D_INNER, D_CONV), D_CONV ** (-0.5)), 'conv_b': jnp.zeros((D_INNER,), jnp.float32), 'x_proj_w': rn(ks[4], (DT_RANK + 2 * D_STATE, D_INNER), D_INNER ** (-0.5)), 'dt_proj_w': rn(ks[5], (D_INNER, DT_RANK), DT_RANK ** (-0.5)), 'dt_proj_b': jnp.full((D_INNER,), -4.6, jnp.float32), 'A_log': jnp.log(jnp.broadcast_to(jnp.arange(1, D_STATE + 1, dtype=jnp.float32), (D_INNER, D_STATE))), 'D': jnp.ones((D_INNER,), jnp.float32), 'out_proj_w': rn(ks[6], (D_MODEL, D_INNER), D_INNER ** (-0.5)), 'fc2_w': rn(ks[7], (D_OUTPUT, D_MODEL), D_MODEL ** (-0.5)), 'fc2_b': jnp.zeros((D_OUTPUT,), jnp.float32)}
    _L1_attn_in = _L1_attn_setup()

    def _L1_ffn_setup():
        import jax, jax.numpy as jnp
        import numpy as np
        TEMPERATURE = 0.5
        CAPACITY_FACTOR = 1.25
        TOP_K = 1
        key = jax.random.key(seed)
        ks = jax.random.split(key, 5)
        B, S, D, H, E = (4, 256, 128, 256, 8)
        s = 0.02
        return {'x': jax.random.normal(ks[0], (B, S, D), jnp.float32), 'gate_w': jax.random.normal(ks[1], (E, D), jnp.float32) * s, 'gate_b': jnp.zeros((E,), jnp.float32), 'rms_w': jnp.ones((E,), jnp.float32), 'w1': jax.random.normal(ks[2], (E, D, H), jnp.float32) * s, 'b1': jnp.zeros((E, H), jnp.float32), 'w2': jax.random.normal(ks[3], (E, H, D), jnp.float32) * s, 'b2': jnp.zeros((E, D), jnp.float32)}
    _L1_ffn_in = _L1_ffn_setup()
    _d = {'L0_attn_x': _L0_attn_in['x'], 'L0_attn_W_Q': _L0_attn_in['W_Q'], 'L0_attn_b_Q': _L0_attn_in['b_Q'], 'L0_attn_W_K': _L0_attn_in['W_K'], 'L0_attn_b_K': _L0_attn_in['b_K'], 'L0_attn_W_V': _L0_attn_in['W_V'], 'L0_attn_b_V': _L0_attn_in['b_V'], 'L0_attn_W_O': _L0_attn_in['W_O'], 'L0_attn_b_O': _L0_attn_in['b_O'], 'L0_ffn_wg_red': _L0_ffn_in['wg_red'], 'L0_ffn_wg': _L0_ffn_in['wg'], 'L0_ffn_w1': _L0_ffn_in['w1'], 'L0_ffn_b1': _L0_ffn_in['b1'], 'L0_ffn_w2': _L0_ffn_in['w2'], 'L0_ffn_b2': _L0_ffn_in['b2'], 'L1_attn_fc1_w': _L1_attn_in['fc1_w'], 'L1_attn_fc1_b': _L1_attn_in['fc1_b'], 'L1_attn_in_proj_w': _L1_attn_in['in_proj_w'], 'L1_attn_conv_w': _L1_attn_in['conv_w'], 'L1_attn_conv_b': _L1_attn_in['conv_b'], 'L1_attn_x_proj_w': _L1_attn_in['x_proj_w'], 'L1_attn_dt_proj_w': _L1_attn_in['dt_proj_w'], 'L1_attn_dt_proj_b': _L1_attn_in['dt_proj_b'], 'L1_attn_A_log': _L1_attn_in['A_log'], 'L1_attn_D': _L1_attn_in['D'], 'L1_attn_out_proj_w': _L1_attn_in['out_proj_w'], 'L1_attn_fc2_w': _L1_attn_in['fc2_w'], 'L1_attn_fc2_b': _L1_attn_in['fc2_b'], 'L1_ffn_gate_w': _L1_ffn_in['gate_w'], 'L1_ffn_gate_b': _L1_ffn_in['gate_b'], 'L1_ffn_rms_w': _L1_ffn_in['rms_w'], 'L1_ffn_w1': _L1_ffn_in['w1'], 'L1_ffn_b1': _L1_ffn_in['b1'], 'L1_ffn_w2': _L1_ffn_in['w2'], 'L1_ffn_b2': _L1_ffn_in['b2']}
    _x0 = _d['L0_attn_x']
    _d['L0_attn_x'] = jax.random.normal(jax.random.fold_in(jax.random.key(seed), 1), (2, 1024, 128), dtype=_x0.dtype)
    del _x0
    return _d

def reference(L0_attn_x, L0_attn_W_Q, L0_attn_b_Q, L0_attn_W_K, L0_attn_b_K, L0_attn_W_V, L0_attn_b_V, L0_attn_W_O, L0_attn_b_O, L0_ffn_wg_red, L0_ffn_wg, L0_ffn_w1, L0_ffn_b1, L0_ffn_w2, L0_ffn_b2, L1_attn_fc1_w, L1_attn_fc1_b, L1_attn_in_proj_w, L1_attn_conv_w, L1_attn_conv_b, L1_attn_x_proj_w, L1_attn_dt_proj_w, L1_attn_dt_proj_b, L1_attn_A_log, L1_attn_D, L1_attn_out_proj_w, L1_attn_fc2_w, L1_attn_fc2_b, L1_ffn_gate_w, L1_ffn_gate_b, L1_ffn_rms_w, L1_ffn_w1, L1_ffn_b1, L1_ffn_w2, L1_ffn_b2):

    def _L0_attn_ref(x, W_Q, b_Q, W_K, b_K, W_V, b_V, W_O, b_O):
        import jax, jax.numpy as jnp
        import numpy as np
        B, T, D = (4, 256, 128)
        H, Dh = (16, 64)
        Q = jnp.einsum('btd,hkd->bthk', x, W_Q) + b_Q
        K = jnp.einsum('btd,hkd->bthk', x, W_K) + b_K
        V = jnp.einsum('btd,hkd->bthk', x, W_V) + b_V
        d_head = W_Q.shape[1]
        scores = jnp.einsum('bqhk,bshk->bhqs', Q, K) / jnp.sqrt(jnp.asarray(d_head, x.dtype))
        attn = jax.nn.softmax(scores, axis=-1)
        out_h = jnp.einsum('bhqs,bshk->bqhk', attn, V)
        return jnp.einsum('bqhk,hdk->bqd', out_h, W_O) + b_O

    def _L0_ffn_ref(hidden_states, wg_red, wg, w1, b1, w2, b2):
        import jax, jax.numpy as jnp
        import numpy as np
        NUM_EXPERTS = 8
        IN_FEATURES = 128
        HIDDEN_FEATURES = 512
        GATE_DIM = 16
        EPS = 0.0001
        b, t, c = hidden_states.shape
        x = hidden_states.reshape(-1, c)
        xr = x @ wg_red.T
        wg_unit = wg / jnp.maximum(jnp.linalg.norm(wg, axis=1, keepdims=True), EPS)
        logits = xr @ wg_unit.T
        gates = jax.nn.softmax(logits, axis=1)
        indices_s = jnp.argmax(gates, axis=1)
        scores = jnp.max(gates, axis=1)
        E = wg.shape[0]
        out = jnp.zeros_like(x)
        for e in range(E):
            mask = (indices_s == e).astype(x.dtype)[:, None]
            h = jax.nn.gelu(x @ w1[e] + b1[e], approximate=False)
            out = out + mask * (h @ w2[e] + b2[e])
        out = out * scores[:, None]
        return out.reshape(b, t, c)

    def _L1_attn_ref(x, fc1_w, fc1_b, in_proj_w, conv_w, conv_b, x_proj_w, dt_proj_w, dt_proj_b, A_log, D, out_proj_w, fc2_w, fc2_b):
        import jax, jax.numpy as jnp
        import numpy as np
        B_SZ, SEQ = (2, 256)
        D_MODEL, D_STATE, D_CONV = (128, 16, 4)
        D_INPUT, D_OUTPUT = (128, 128)
        D_INNER = 2 * D_MODEL
        DT_RANK = D_MODEL // 16
        B, L, _ = x.shape
        d_inner, d_conv = conv_w.shape
        d_state = A_log.shape[1]
        dt_rank = dt_proj_w.shape[1]
        h = x @ fc1_w.T + fc1_b
        xz = h @ in_proj_w.T
        xc, z = jnp.split(xz, 2, axis=-1)
        xp = jnp.pad(xc, ((0, 0), (d_conv - 1, 0), (0, 0)))
        u = sum((xp[:, w:w + L, :] * conv_w[:, w] for w in range(d_conv))) + conv_b
        u = jax.nn.silu(u)
        x_dbl = u @ x_proj_w.T
        dt_low, Bm, Cm = jnp.split(x_dbl, [dt_rank, dt_rank + d_state], axis=-1)
        dt = jax.nn.softplus(dt_low @ dt_proj_w.T + dt_proj_b)
        A = -jnp.exp(A_log)

        def step(hstate, t):
            dt_t, B_t, C_t, u_t = t
            dA = jnp.exp(dt_t[..., None] * A)
            hstate = dA * hstate + (dt_t * u_t)[..., None] * B_t[:, None, :]
            y_t = jnp.einsum('bdn,bn->bd', hstate, C_t)
            return (hstate, y_t)
        h0 = jnp.zeros((B, d_inner, d_state), x.dtype)
        xs = (jnp.swapaxes(dt, 0, 1), jnp.swapaxes(Bm, 0, 1), jnp.swapaxes(Cm, 0, 1), jnp.swapaxes(u, 0, 1))
        _, ys = jax.lax.scan(step, h0, xs)
        y = jnp.swapaxes(ys, 0, 1) + u * D
        y = y * jax.nn.silu(z)
        out = y @ out_proj_w.T
        return out @ fc2_w.T + fc2_b

    def _L1_ffn_ref(x, gate_w, gate_b, rms_w, w1, b1, w2, b2):
        import jax, jax.numpy as jnp
        import numpy as np
        TEMPERATURE = 0.5
        CAPACITY_FACTOR = 1.25
        TOP_K = 1
        B, S, D = x.shape
        E = gate_w.shape[0]
        xf = x.reshape(-1, D)
        N = xf.shape[0]
        logits = xf @ gate_w.T + gate_b
        eps = jnp.finfo(logits.dtype).eps
        ms = jnp.mean(logits * logits, axis=-1, keepdims=True)
        logits = logits * jax.lax.rsqrt(ms + eps) * rms_w
        gates = jax.nn.softmax(logits / TEMPERATURE, axis=-1)
        g, idx = jax.lax.top_k(gates, TOP_K)
        g, idx = (g[:, 0], idx[:, 0])
        capacity = min(int(np.ceil(N * TOP_K / E * CAPACITY_FACTOR)), N)
        counts = jnp.zeros((E,), jnp.int32).at[idx].add(1)
        active = (counts > 0) & (capacity >= 1)
        mask = active[idx].astype(gates.dtype)
        masked = g * mask
        norm_g = masked / (masked + 1e-06)
        h = jax.nn.gelu(jnp.einsum('nd,edh->neh', xf, w1) + b1, approximate=False)
        y = jnp.einsum('neh,ehd->ned', h, w2) + b2
        out = (y * norm_g[:, None, None]).sum(axis=1)
        return out.reshape(B, S, D)
    x = L0_attn_x
    x = x + _L0_attn_ref(_layernorm(x, axis=-1), L0_attn_W_Q, L0_attn_b_Q, L0_attn_W_K, L0_attn_b_K, L0_attn_W_V, L0_attn_b_V, L0_attn_W_O, L0_attn_b_O)
    x = x + _L0_ffn_ref(_layernorm(x, axis=-1), L0_ffn_wg_red, L0_ffn_wg, L0_ffn_w1, L0_ffn_b1, L0_ffn_w2, L0_ffn_b2)
    x = x + _L1_attn_ref(_layernorm(x, axis=-1), L1_attn_fc1_w, L1_attn_fc1_b, L1_attn_in_proj_w, L1_attn_conv_w, L1_attn_conv_b, L1_attn_x_proj_w, L1_attn_dt_proj_w, L1_attn_dt_proj_b, L1_attn_A_log, L1_attn_D, L1_attn_out_proj_w, L1_attn_fc2_w, L1_attn_fc2_b)
    x = x + _L1_ffn_ref(_layernorm(x, axis=-1), L1_ffn_gate_w, L1_ffn_gate_b, L1_ffn_rms_w, L1_ffn_w1, L1_ffn_b1, L1_ffn_w2, L1_ffn_b2)
    return x

_drawn_inputs = setup_inputs


def setup_inputs(seed=0):
    import zlib

    import numpy as np

    out = dict(_drawn_inputs(seed))
    spreads = {'L0_attn_b_Q': (0.0, 0.1),
     'L0_attn_b_K': (0.0, 0.1),
     'L0_attn_b_V': (0.0, 0.1),
     'L0_attn_b_O': (0.0, 0.1),
     'L1_attn_fc1_b': (0.0, 0.1),
     'L1_attn_conv_b': (0.0, 0.1),
     'L1_attn_dt_proj_b': (-4.599999904632568, 0.2),
     'L1_attn_D': (1.0, 0.2),
     'L1_attn_fc2_b': (0.0, 0.1),
     'L1_ffn_gate_b': (0.0, 0.1),
     'L1_ffn_rms_w': (1.0, 0.2),
     'L1_ffn_b1': (0.0, 0.1),
     'L1_ffn_b2': (0.0, 0.1)}
    factors = {}
    for name, (base, spread) in spreads.items():
        noise = np.random.default_rng([zlib.crc32(name.encode()), seed]).standard_normal(out[name].shape)
        drawn = base * np.exp(spread * noise) if base else spread * noise
        out[name] = jnp.asarray(drawn.astype(out[name].dtype))
    for name, factor in factors.items():
        out[name] = (out[name] * factor).astype(out[name].dtype)
    return out
```

```python
from contextlib import ExitStack

import numpy as np

import concourse.bass as bass
from concourse import mybir

F32 = mybir.dt.float32
F32R = mybir.dt.float32r
ACT = mybir.ActivationFunctionType
ALU = mybir.AluOpType
AXX = mybir.AxisListType.X

P = 128
B, SEQ, D = 2, 1024, 128
NT = SEQ // P
CH = 512
NC = SEQ // CH
H, DH = 16, 64
NPAIR = H // 2
E0, F0, GATE = 8, 512, 16
M0 = F0 // P
DI, NS, DTR, DCONV = 256, 16, 8, 4
KI = DI // P
E1, F1 = 8, 256
M1 = E1 * F1 // P
LO = 64
LN_EPS, NORM_EPS, GATE_EPS = 1e-5, 1e-4, 1e-6
F32_EPS = float(np.finfo(np.float32).eps)


class Progress:

    def __init__(self, sem, step=1):
        self.sem, self.step, self.count = sem, step, 0

    def mark(self, instruction):
        instruction.then_inc(self.sem, self.step)
        self.count += self.step
        return (self, self.count)


class Waits:

    def __init__(self):
        self.seen = {}

    def __call__(self, engine, *marks):
        for m in marks:
            if m is None:
                continue
            if isinstance(m, list):
                self(engine, *m)
                continue
            progress, level = m
            key = (id(engine), progress)
            if self.seen.get(key, 0) < level:
                engine.wait_ge(progress.sem, level)
                self.seen[key] = level


class Ring:

    def __init__(self, buffers):
        self.buffers, self.free, self.at = buffers, [[] for _ in buffers], -1

    def take(self):
        self.at = (self.at + 1) % len(self.buffers)
        return self.at, self.buffers[self.at]


def two_layer_program(nc, a, out):
    pe, act, dve, pool, sp = nc.tensor, nc.scalar, nc.vector, nc.gpsimd, nc.sync
    wait = Waits()
    with ExitStack() as ctx:
        def sb(name, shape, dt=F32, scope=ctx):
            return scope.enter_context(nc.sbuf_tensor(name, shape, dt))

        def progress(name, step=1):
            return Progress(ctx.enter_context(nc.semaphore(name)), step)

        pe_p, act_p, dve_p, pool_p = (progress(n) for n in ("pe_done", "act_done", "dve_done", "pool_done"))

        def pool_alone():
            wait(pool, (pool_p, pool_p.count))

        def pool_set(dst, value):
            pool_alone()
            return pool_p.mark(pool.memset(dst, value))

        psum = ctx.enter_context(nc.psum_tensor("psum", [P, 8 * CH], F32))

        def banks(first, n=1):
            return psum[:, first * CH:(first + n) * CH]

        work = Ring([banks(0), banks(1)])

        def load(name, dst, src):
            return progress("ld_" + name, 16).mark(sp.dma_start(dst, src))

        x = sb("x", [P, B * NT, D])
        xnT = sb("xnT", [P, B, SEQ])
        ident = sb("ident", [P, P])
        xn = sb("xn", [P, NT, D])
        stats = sb("stats", [P, NT, 6])
        mv = sb("mv", [P, NT, 2])
        rstd = sb("rstd", [P, NT])
        std = sb("std", [P, NT])
        x_d = a["x"].rearrange("(t p) d -> p t d", p=P)
        out_d = out.rearrange("(t p) d -> p t d", p=P)
        ld_x = [load(f"x{b}", x[:, b * NT:(b + 1) * NT, :], x_d[:, b * NT:(b + 1) * NT, :]) for b in range(B)]
        ld_ident = load("ident", ident[:, :], a["ident"])
        x_mark = list(ld_x)
        xnT_mark = [[], []]
        xnT_free = [[], []]
        ln_free = []

        def layer_norm(b):
            nonlocal ln_free
            wait(dve, x_mark[b], *ln_free)
            for t in range(NT):
                m = dve_p.mark(dve.bn_stats(stats[:, t, :], x[:, b * NT + t, :]))
            wait(dve, m)
            for t in range(NT):
                m = dve_p.mark(dve.bn_aggr(mv[:, t, :], stats[:, t, :]))
            wait(dve, m)
            m = dve_p.mark(dve.tensor_scalar(std[:, :], mv[:, :, 1], LN_EPS, None, ALU.add))
            wait(act, m)
            m = act_p.mark(act.activation(std[:, :], std[:, :], ACT.Sqrt))
            wait(dve, m)
            m = dve_p.mark(dve.reciprocal(rstd[:, :], std[:, :]))
            wait(dve, m)
            rows = []
            for t in range(NT):
                rows.append(dve_p.mark(dve.tensor_scalar(
                    xn[:, t, :], x[:, b * NT + t, :], mv[:, t, 0:1], rstd[:, t:t + 1], ALU.subtract, ALU.mult)))
            ends = []
            for g in range(NT // 4):
                i, bank = work.take()
                wait(pe, rows[4 * g + 3], ld_ident, *work.free[i])
                for t in range(4):
                    ins = pe.transpose(bank[:, t * P:(t + 1) * P], xn[:, 4 * g + t, :], ident[:, :])
                m = pe_p.mark(ins)
                wait(act, m, *xnT_free[b])
                ends.append(act_p.mark(act.copy(xnT[:, b, g * CH:(g + 1) * CH], bank)))
                work.free[i] = [ends[-1]]
            ln_free = [m]
            xnT_mark[b] = [ends[-1]]
            xnT_free[b] = []

        with ExitStack() as scope:
            def sba(name, shape, dt=F32):
                return sb(name, shape, dt, scope)

            wq, wk = (sba(n, [P, H, 2, DH]) for n in ("wq", "wk"))
            wv, wo = (sba(n, [P, H * DH]) for n in ("wv", "wo"))
            bq, bk = sba("bq", [P, H]), sba("bk", [P, H])
            bv, bo = sba("bv", [P, H * DH]), sba("bo", [P, D])
            ones = sba("ones", [P, 1])
            sel = sba("sel", [P, NT, P])
            V = sba("V", [P, NT, H * DH])
            K1, K2, Q1, Q2 = ([[sba(f"{n}{q}{s}", [P, SEQ], F32R) for s in range(2)] for q in range(2)]
                              for n in ("K1_", "K2_", "Q1_", "Q2_"))
            NPB = 3
            prob = [Ring([sba(f"prob{s}{i}", [P, SEQ]) for i in range(NPB)]) for s in range(2)]
            psums = [[sba(f"psums{q}{s}", [P, SEQ]) for s in range(2)] for q in range(2)]
            mx = sba("mx", [P, 2, NT, NC])
            nmx = sba("nmx", [P, P])
            mrow = sba("mrow", [P, P], F32R)
            rs = sba("rs", [P, P])
            rsT = sba("rsT", [P, P])
            oraw = sba("oraw", [P, SEQ])
            onorm = sba("onorm", [P, SEQ])

            ld_wk, ld_wq = ([load(f"{n}{k}", w[:, :, k, :], a[n].rearrange("d (h k) -> d h k", h=H)) for k in range(2)]
                            for n, w in (("wk", wk), ("wq", wq)))
            ld_b = [load("bk", bk[:, :], a["bk"]), load("bq", bq[:, :], a["bq"])]
            ld_wv = [load("wv", wv[:, :], a["wv"]), load("bv", bv[:, :], a["bv"].partition_broadcast(P))]
            ld_wo = [load("wo", wo[:, :], a["wo"]), load("bo", bo[:, :], a["bo"].partition_broadcast(P))]
            ld_sel = load("sel", sel[:, :, :], a["sel"])

            for q in range(2):
                for s in range(2):
                    pool_set(Q2[q][s][LO:P, :].bitcast(F32), 0.0)
                    pool_set(K2[q][s][LO:P, :].bitcast(F32), 0.0)
            pool_set(ones[:, :], 1.0)
            for z in (nmx, rs):
                init = pool_set(z[:, :], 0.0)
            wait(pool, init)
            for q in range(2):
                for s in range(2):
                    init = pool_set(K2[q][s][LO:LO + 1, :].bitcast(F32), 1.0)

            guard = [[progress(f"guard{q}{s}", 16) for s in range(2)] for q in range(2)]
            guard_mark = [[None, None], [None, None]]
            qk_mark = [[{}, {}], [{}, {}]]
            score_mark = [[], []]
            S = [banks(2, 2), banks(4, 2)]
            S_free = [[], []]
            O = banks(6, 2)
            O_free = []
            oraw_free, onorm_free, rsT_free, rs_free = [], [], [], []
            mx_free, nmx_free, mrow_free = [], [], []
            psums_mark, psums_free = [[None, None], [None, None]], [[], []]
            prob_mark = {}
            pv_end = {}
            V_mark = [None]
            V_free = []

            def values(b):
                for t in range(NT):
                    for c in range(2):
                        i, bank = work.take()
                        wait(pe, xnT_mark[b], ld_wv, work.free[i])
                        m = pe_p.mark(pe.matmul(bank, xnT[:, b, t * P:(t + 1) * P], wv[:, c * CH:(c + 1) * CH],
                                                start=True, stop=True))
                        wait(dve, m, ld_wv, V_free)
                        V_mark[0] = dve_p.mark(dve.tensor_tensor(V[:, t, c * CH:(c + 1) * CH], bank,
                                                                 bv[:, c * CH:(c + 1) * CH], ALU.add))
                        work.free[i] = [V_mark[0]]

            def project(pair, s, kind, c):
                b, p = divmod(pair, NPAIR)
                q, h = pair % 2, 2 * p + s
                w, bias, full, part = (wk, bk, K1, K2) if kind == "k" else (wq, bq, Q1, Q2)
                full, part = full[q][s], part[q][s]
                cs = slice(c * CH, (c + 1) * CH)
                i, bank = work.take()
                wait(pe, xnT_mark[b], ld_wk, ld_wq, work.free[i])
                twice = w[:, h, :, :].rearrange("d r k -> d (r k)")
                m = pe_p.mark(pe.matmul(bank, twice, xnT[:, b, cs], start=True, stop=True))
                wait(act, m, ld_b, score_mark[q])
                hi = act_p.mark(act.activation(full[:, cs], bank, ACT.Identity, bias=bias[:, h:h + 1]))
                wait(dve, m, hi, ld_b, score_mark[q], init)
                if kind == "k":
                    wait(act, init)
                    hi2 = act_p.mark(act.activation(part[0:LO, cs], bank[0:LO, :], ACT.Identity,
                                                    bias=bias[0:LO, h:h + 1]))
                    lo = dve_p.mark(dve.scalar_tensor_tensor(
                        out=full[LO:P, cs], in0=bank[LO:P, :], scalar=bias[LO:P, h:h + 1],
                        in1=full[LO:P, cs], op0=ALU.add, op1=ALU.subtract))
                    marks = [hi2, lo]
                else:
                    lo = dve_p.mark(dve.scalar_tensor_tensor(
                        out=part[0:LO, cs], in0=bank[0:LO, :], scalar=bias[0:LO, h:h + 1],
                        in1=full[0:LO, cs], op0=ALU.add, op1=ALU.subtract))
                    marks = [hi, lo]
                work.free[i] = marks
                qk_mark[q][s][kind, c] = marks

            def row_max(pair, s, t):
                q = pair % 2
                for c in range(NC):
                    i, bank = work.take()
                    wait(pe, list(qk_mark[q][s].values()), work.free[i])
                    m = pe_p.mark(pe.matmul(bank, Q1[q][s][:, t * P:(t + 1) * P], K1[q][s][:, c * CH:(c + 1) * CH],
                                            start=True, stop=True))
                    wait(dve, m, mx_free)
                    r = dve_p.mark(dve.tensor_reduce(mx[:, s, t, c:c + 1], bank, AXX, ALU.max))
                    work.free[i] = [r]
                return r

            def guard_rows(pair, last_max):
                nonlocal mx_free, nmx_free, mrow_free
                q = pair % 2
                wait(dve, last_max, nmx_free, init)
                m = dve_p.mark(dve.tensor_reduce(nmx[:, 0:2 * NT], mx[:, :, :, :].rearrange("p s t c -> p (s t) c"),
                                                 AXX, ALU.max, negate=True))
                mx_free = [m]
                i, bank = work.take()
                wait(pe, m, ld_ident, work.free[i])
                m = pe_p.mark(pe.transpose(bank[:, 0:P], nmx[:, :], ident[:, :]))
                nmx_free = [m]
                wait(dve, m, mrow_free)
                m = dve_p.mark(dve.tensor_copy(mrow[0:2 * NT, :], bank[0:2 * NT, 0:P]))
                work.free[i] = [m]
                wait(sp, m, score_mark[q], init)
                mrow_free = []
                for s in range(2):
                    guard_mark[q][s] = guard[q][s].mark(sp.dma_start(
                        Q2[q][s][LO:LO + 1, :].rearrange("o (t k) -> o t k", t=NT).bitcast(F32),
                        mrow[s * NT:(s + 1) * NT, :].bitcast(F32)))
                    mrow_free.append(guard_mark[q][s])

            def scores(pair, j, s):
                q = pair % 2
                ks = slice(j * P, (j + 1) * P)
                wait(pe, list(qk_mark[q][s].values()), S_free[s])
                for c in range(NC):
                    pe.matmul(S[s][:, c * CH:(c + 1) * CH], K1[q][s][:, ks], Q1[q][s][:, c * CH:(c + 1) * CH],
                              start=True, stop=False)
                wait(pe, guard_mark[q][s], init)
                for c in range(NC):
                    ins = pe.matmul(S[s][:, c * CH:(c + 1) * CH], K2[q][s][:, ks], Q2[q][s][:, c * CH:(c + 1) * CH],
                                    start=False, stop=True)
                m = pe_p.mark(ins)
                score_mark[q] = [m]
                i, weights = prob[s].take()
                wait(act, m, prob[s].free[i])
                e = act_p.mark(act.activation(weights[:, :], S[s], ACT.Exp, scale=float(DH) ** -0.5))
                S_free[s] = [e]
                prob_mark[pair, j, s] = (i, e)
                if j == 0:
                    return
                total = psums[q][s]
                before = prob[s].buffers[prob_mark[pair, 0, s][0]] if j == 1 else total
                wait(pool, e, prob_mark[pair, 0, s][1], psums_free[q], psums_mark[q][s])
                pool_alone()
                psums_mark[q][s] = pool_p.mark(pool.tensor_tensor(total[:, :], before[:, :], weights[:, :], ALU.add))
                if j == 1:
                    prob[s].free[prob_mark[pair, 0, s][0]].append(psums_mark[q][s])
                prob[s].free[i] = [psums_mark[q][s]]

            def weighted_values(pair, j):
                nonlocal O_free
                p = pair % NPAIR
                slots = [prob_mark[pair, j, s] for s in range(2)]
                wait(pe, V_mark[0], *(e for _, e in slots))
                if j == 0:
                    wait(pe, O_free)
                for c in range(NC):
                    for s in range(2):
                        h = 2 * p + s
                        ins = pe.matmul(O[s * LO:(s + 1) * LO, c * CH:(c + 1) * CH], V[:, j, h * DH:(h + 1) * DH],
                                        prob[s].buffers[slots[s][0]][:, c * CH:(c + 1) * CH],
                                        start=(j == 0), stop=(j == NT - 1))
                m = pe_p.mark(ins)
                for s in range(2):
                    prob[s].free[slots[s][0]] = prob[s].free[slots[s][0]] + [m]
                if j == NT - 1:
                    pv_end[pair] = m

            def take_out(pair):
                nonlocal O_free
                wait(act, pv_end[pair], oraw_free)
                O_free = [act_p.mark(act.copy(oraw[:, :], O))]

            def inverse_sums(pair):
                nonlocal rs_free, rsT_free
                q = pair % 2
                i, bank = work.take()
                wait(pe, psums_mark[q], work.free[i], init)
                for s in range(2):
                    for t in range(NT):
                        ins = pe.matmul(bank[:, s * NT + t:s * NT + t + 1], psums[q][s][:, t * P:(t + 1) * P],
                                        ones[:, :], start=True, stop=True)
                m = pe_p.mark(ins)
                psums_free[q] = [m]
                wait(dve, m, rs_free, init)
                m = dve_p.mark(dve.reciprocal(rs[:, 0:2 * NT], bank[:, 0:2 * NT]))
                work.free[i] = [m]
                i, bank = work.take()
                wait(pe, m, ld_ident, work.free[i])
                m = pe_p.mark(pe.transpose(bank[:, 0:P], rs[:, :], ident[:, :]))
                rs_free = [m]
                wait(dve, m, rsT_free)
                m = dve_p.mark(dve.tensor_copy(rsT[:, :], bank[:, 0:P]))
                work.free[i] = [m]
                return m

            def project_out(pair, rsT_mark):
                nonlocal rsT_free, onorm_free, oraw_free
                b, p = divmod(pair, NPAIR)
                for c in range(NC):
                    i, bank = work.take()
                    wait(pe, rsT_mark, ld_sel, work.free[i])
                    for t in range(4):
                        ins = pe.matmul(bank[:, t * P:(t + 1) * P], sel[:, 4 * c + t, :], rsT[:, :],
                                        start=True, stop=True)
                    m = pe_p.mark(ins)
                    wait(dve, m, O_free, onorm_free)
                    n = dve_p.mark(dve.tensor_tensor(onorm[:, c * CH:(c + 1) * CH], bank,
                                                     oraw[:, c * CH:(c + 1) * CH], ALU.mult))
                    work.free[i] = [n]
                rsT_free, oraw_free = [m], [n]
                for c in range(NC):
                    i, bank = work.take()
                    wait(pe, n, ld_wo, work.free[i])
                    for t in range(4):
                        ins = pe.matmul(bank[:, t * P:(t + 1) * P], onorm[:, (4 * c + t) * P:(4 * c + t + 1) * P],
                                        wo[:, p * D:(p + 1) * D], start=True, stop=True)
                    m = pe_p.mark(ins)
                    wait(dve, m, x_mark[b])
                    xs = x[:, b * NT + 4 * c:b * NT + 4 * c + 4, :]
                    r = dve_p.mark(dve.tensor_tensor(xs, bank.rearrange("p (t d) -> p t d", d=D), xs, ALU.add))
                    work.free[i] = [r]
                onorm_free = [m]
                x_mark[b] = r

            for b in range(B):
                layer_norm(b)
                wait(dve, ld_wo)
                xs = x[:, b * NT:(b + 1) * NT, :]
                wait(dve, dve_mark_of(x_mark, b, dve_p))
                x_mark[b] = dve_p.mark(dve.tensor_tensor(
                    xs, xs, bo[:, :].unsqueeze(1).broadcast_to([P, NT, D]), ALU.add))

            pieces = [(s, kind, c) for s in range(2) for kind in "kq" for c in range(NC)]
            tiles = [(s, t) for t in range(NT) for s in range(2)]
            for piece in pieces:
                project(0, *piece)
            for s, t in tiles:
                last = row_max(0, s, t)
            guard_rows(0, last)
            values(0)
            npairs = B * NPAIR
            for pair in range(npairs + 1):
                for j in range(NT):
                    if pair < npairs:
                        for s in range(2):
                            scores(pair, j, s)
                    nxt = pair + 1
                    if nxt < npairs:
                        if j < 3:
                            for piece in pieces[3 * j:3 * j + 3]:
                                project(nxt, *piece)
                        elif j < 7:
                            for s, t in tiles[4 * (j - 3):4 * (j - 3) + 4]:
                                last = row_max(nxt, s, t)
                        else:
                            guard_rows(nxt, last)
                    if j > 0 and pair < npairs:
                        weighted_values(pair, j - 1)
                    if j == 0 and pair > 0:
                        weighted_values(pair - 1, NT - 1)
                        take_out(pair - 1)
                        if pair == NPAIR:
                            V_free = [pv_end[pair - 1]]
                            values(1)
                    if j == 1 and pair > 0:
                        rsT_mark = inverse_sums(pair - 1)
                    if j == 2 and pair > 0:
                        project_out(pair - 1, rsT_mark)

        def barrier():
            ends = [(p, p.count) for p in (pe_p, act_p, dve_p, pool_p)]
            for engine in (pe, act, dve, pool, sp):
                wait(engine, ends)

        barrier()
        hid = Ring([banks(i) for i in range(2, 6)])
        ybank = Ring([banks(6), banks(7)])

        def tile_bank(bank):
            return bank.rearrange("p (t d) -> p t d", d=D)

        with ExitStack() as scope:
            def sba(name, shape, dt=F32):
                return sb(name, shape, dt, scope)

            w1, w2 = sba("e0_w1", [P, E0, F0]), sba("e0_w2", [P, E0, M0, D])
            b1 = sba("e0_b1", [P, E0 * M0])
            b2 = sba("e0_b2", [P, NT, D])
            wred = sba("e0_wred", [P, P])
            wg, wgsq = sba("e0_wg", [P, P]), sba("e0_wgsq", [E0, GATE])
            wgn = sba("e0_wgn", [E0, 1])
            wgu = sba("e0_wgu", [P, E0])
            rank = sba("e0_rank", [P, E0])
            xrT = sba("e0_xrT", [P, SEQ])
            lg, ex, one = (sba(f"e0_{n}", [P, NT, E0]) for n in ("logits", "exps", "onehot"))
            coef = sba("e0_coef", [P, P])
            coefT = sba("e0_coefT", [P, P])
            top, score = sba("e0_top", [P, NT]), sba("e0_score", [P, NT])
            hT = Ring([sba(f"e0_h{i}", [P, M0, CH]) for i in range(2)])

            z0 = pool_set(wg[:, :], 0.0)
            pool_set(b2[:, :, :], 0.0)
            z1 = pool_set(coef[:, :], 0.0)
            ld_g = [load("e0_wred", wred[:, :], a["e0_wred"]),
                    load("e0_rank", rank[:, :], a["rank"].partition_broadcast(P))]
            wait(sp, z0)
            ld_wg = load("e0_wg", wg[0:E0, 0:GATE], a["e0_wg"])
            ld_w1 = [load(f"e0_w1{e}", w1[:, e, :], a["e0_w1"][e]) for e in range(E0)]
            ld_w2 = [load(f"e0_w2{e}", w2[:, e, :, :], a["e0_w2"][e].rearrange("(m p) d -> p m d", p=P))
                     for e in range(E0)]
            ld_b1 = load("e0_b1", b1[:, :], a["e0_b1"])
            wait(sp, z1)
            ld_b2 = [load(f"e0_b2{t}", b2[E0 * t:E0 * (t + 1), t, :], a["e0_b2"]) for t in range(NT)]

            wait(dve, ld_wg)
            m = dve_p.mark(dve.tensor_tensor(wgsq[:, :], wg[0:E0, 0:GATE], wg[0:E0, 0:GATE], ALU.mult))
            wait(dve, m)
            m = dve_p.mark(dve.tensor_reduce(wgn[:, :], wgsq[:, :], AXX, ALU.add))
            wait(act, m)
            m = act_p.mark(act.activation(wgn[:, :], wgn[:, :], ACT.Sqrt))
            wait(dve, m)
            m = dve_p.mark(dve.tensor_scalar(wgn[:, :], wgn[:, :], NORM_EPS, None, ALU.max))
            wait(dve, m)
            m = dve_p.mark(dve.reciprocal(wgn[:, :], wgn[:, :]))
            wait(dve, m)
            m = dve_p.mark(dve.tensor_scalar(wg[0:E0, 0:GATE], wg[0:E0, 0:GATE], wgn[:, 0:1], None, ALU.mult))
            i, bank = work.take()
            wait(pe, m, z0, work.free[i])
            m = pe_p.mark(pe.transpose(bank[:, 0:P], wg[:, :], ident[:, :]))
            wait(dve, m)
            wgu_mark = dve_p.mark(dve.tensor_copy(wgu[:, :], bank[:, 0:E0]))
            work.free[i] = [wgu_mark]
            gate_free = []

            def experts0(b):
                nonlocal gate_free
                layer_norm(b)
                for c in range(NC):
                    i, bank = work.take()
                    wait(pe, xnT_mark[b], ld_g, work.free[i])
                    m = pe_p.mark(pe.matmul(bank, wred[:, :], xnT[:, b, c * CH:(c + 1) * CH], start=True, stop=True))
                    wait(act, m, gate_free)
                    m = act_p.mark(act.copy(xrT[:, c * CH:(c + 1) * CH], bank))
                    work.free[i] = [m]
                i, bank = work.take()
                wait(pe, m, wgu_mark, work.free[i])
                for t in range(NT):
                    ins = pe.matmul(bank[:, t * E0:(t + 1) * E0], xrT[:, t * P:(t + 1) * P], wgu[:, :],
                                    start=True, stop=True)
                m = pe_p.mark(ins)

                def wide(v):
                    return v[:, :].unsqueeze(2).broadcast_to([P, NT, E0])

                flat = bank[:, 0:NT * E0].rearrange("p (t e) -> p t e", e=E0)
                wait(dve, m, gate_free)
                m = dve_p.mark(dve.tensor_reduce(top[:, :], flat, AXX, ALU.max))
                wait(dve, m)
                m = dve_p.mark(dve.tensor_tensor(lg[:, :, :], flat, wide(top), ALU.subtract))
                work.free[i] = [m]
                wait(act, m)
                n = act_p.mark(act.activation(ex[:, :, :], lg[:, :, :], ACT.Exp))
                wait(dve, m, ld_g)
                m = dve_p.mark(dve.tensor_scalar(one[:, :, :], lg[:, :, :], 0.0, None, ALU.is_equal))
                wait(dve, m)
                m = dve_p.mark(dve.tensor_tensor(one[:, :, :], one[:, :, :],
                                                 rank[:, :].unsqueeze(1).broadcast_to([P, NT, E0]), ALU.mult))
                wait(dve, m)
                m = dve_p.mark(dve.tensor_reduce(top[:, :], one[:, :, :], AXX, ALU.max))
                wait(dve, m)
                m = dve_p.mark(dve.tensor_tensor(one[:, :, :], one[:, :, :], wide(top), ALU.is_equal))
                wait(dve, n)
                m = dve_p.mark(dve.tensor_reduce(score[:, :], ex[:, :, :], AXX, ALU.add))
                wait(dve, m)
                m = dve_p.mark(dve.reciprocal(score[:, :], score[:, :]))
                wait(dve, m, z1)
                cview = coef[:, 0:NT * E0].rearrange("p (t e) -> p t e", e=E0)
                coef_mark = dve_p.mark(dve.tensor_tensor(cview, one[:, :, :], wide(score), ALU.mult))
                i, bank = work.take()
                wait(pe, coef_mark, work.free[i])
                m = pe_p.mark(pe.transpose(bank[:, 0:P], coef[:, :], ident[:, :]))
                wait(dve, m)
                m = dve_p.mark(dve.tensor_copy(coefT[:, :], bank[:, 0:P]))
                work.free[i] = [m]
                for c in range(NC):
                    i, bank = work.take()
                    wait(pe, m, ld_b2, work.free[i])
                    for t in range(4):
                        ins = pe.matmul(bank[:, t * P:(t + 1) * P], coefT[:, :], b2[:, 4 * c + t, :],
                                        start=True, stop=True)
                    n = pe_p.mark(ins)
                    xs = x[:, b * NT + 4 * c:b * NT + 4 * c + 4, :]
                    wait(dve, n)
                    x_mark[b] = dve_p.mark(dve.tensor_tensor(xs, tile_bank(bank), xs, ALU.add))
                    work.free[i] = [x_mark[b]]

                def hidden(e, c):
                    k, h = hT.take()
                    for m_ in range(M0):
                        i, bank = hid.take()
                        wait(pe, ld_w1[e], hid.free[i])
                        m = pe_p.mark(pe.matmul(bank, w1[:, e, m_ * P:(m_ + 1) * P], xnT[:, b, c * CH:(c + 1) * CH],
                                                start=True, stop=True))
                        wait(act, m, ld_b1, hT.free[k])
                        g = act_p.mark(act.activation(h[:, m_, :], bank, ACT.Gelu,
                                                      bias=b1[:, e * M0 + m_:e * M0 + m_ + 1]))
                        hid.free[i] = [g]
                    xnT_free[b] = [m]
                    return k, h, g

                def down(e, c, k, h, g):
                    i, bank = ybank.take()
                    wait(pe, g, ld_w2[e], ybank.free[i])
                    for t in range(4):
                        for m_ in range(M0):
                            ins = pe.matmul(bank[:, t * P:(t + 1) * P], h[:, m_, t * P:(t + 1) * P], w2[:, e, m_, :],
                                            start=(m_ == 0), stop=(m_ == M0 - 1))
                    m = pe_p.mark(ins)
                    hT.free[k] = [m]
                    for t in range(4):
                        tt = 4 * c + t
                        xs = x[:, b * NT + tt, :]
                        wait(dve, m, x_last[tt])
                        x_last[tt] = dve_p.mark(dve.scalar_tensor_tensor(
                            out=xs, in0=bank[:, t * P:(t + 1) * P], scalar=coef[:, tt * E0 + e:tt * E0 + e + 1],
                            in1=xs, op0=ALU.mult, op1=ALU.add))
                    ybank.free[i] = [x_last[tt]]

                x_last = [x_mark[b]] * NT
                todo = [(e, c) for e in range(E0) for c in range(NC)]
                held = None
                for unit in todo:
                    new = (*unit, *hidden(*unit))
                    if held:
                        down(*held)
                    held = new
                down(*held)
                x_mark[b] = x_last[NT - 1]
                gate_free = [x_mark[b]]

            for b in range(B):
                experts0(b)
        barrier()

        with ExitStack() as scope:
            def sba(name, shape, dt=F32):
                return sb(name, shape, dt, scope)

            HS = 64
            PAD = DCONV - 1
            fc1, inp = sba("fc1", [P, D]), sba("inp", [P, 2 * DI])
            fc1b = sba("fc1b", [P, 1])
            cw, cb = sba("cw", [P, KI, DCONV]), sba("cb", [P, KI])
            xpj = sba("xpj", [P, KI, P])
            dtp, dtb = sba("dtp", [P, DI]), sba("dtb", [P, KI])
            alog, dsk = sba("alog", [P, KI, NS]), sba("dsk", [P, KI])
            outp, fc2, fc2b = sba("outp", [P, KI, D]), sba("fc2", [P, D]), sba("fc2b", [P, D])
            pick = sba("pick", [P, 2 * NS, P])
            pickr = sba("pickr", [P, 2 * NS, P], F32R)
            h1T = sba("h1T", [P, SEQ])
            xc = sba("xc", [P, KI, PAD + SEQ])
            u, dt, du, zg = (sba(n, [P, KI, SEQ]) for n in ("u", "dt", "du", "zg"))
            xd = sba("xd", [P, SEQ])
            xdr = sba("xdr", [P, SEQ], F32R)
            tmp1, tmp2 = sba("tmp1", [P, SEQ]), sba("tmp2", [P, SEQ])
            dA = Ring([sba(f"dA{i}", [P, SEQ]) for i in range(2)])
            dBu = Ring([sba(f"dBu{i}", [P, SEQ]) for i in range(2)])
            hs = Ring([sba(f"hs{i}", [P, SEQ]) for i in range(2)])
            hc = Ring([sba(f"hc{i}", [P, SEQ]) for i in range(3)])
            cc = Ring([sba(f"cc{i}", [P, SEQ]) for i in range(2)])
            bb = Ring([banks(2, 2)])

            z = pool_set(xc[:, :, 0:PAD], 0.0)
            ld = {}
            for name, t in (("fc1", fc1), ("fc1b", fc1b), ("inp", inp), ("cw", cw), ("cb", cb), ("xpj", xpj),
                            ("dtp", dtp), ("dtb", dtb), ("alog", alog), ("dsk", dsk), ("outp", outp), ("fc2", fc2),
                            ("pick", pick)):
                ld[name] = load("s_" + name, t[:], a[name])
            ld["fc2b"] = load("s_fc2b", fc2b[:, :], a["fc2b"].partition_broadcast(P))
            wait(dve, ld["pick"])
            pick_mark = dve_p.mark(dve.tensor_copy(pickr[:, :, :], pick[:, :, :]))
            wait(act, ld["alog"])
            A_mark = act_p.mark(act.activation(alog[:, :, :], alog[:, :, :], ACT.Exp))
            wait(dve, A_mark)
            A_mark = dve_p.mark(dve.tensor_scalar(alog[:, :, :], alog[:, :, :], -1.0, None, ALU.mult))
            phase_free = []

            def selective_scan(b):
                nonlocal phase_free
                layer_norm(b)
                for c in range(NC):
                    i, bank = work.take()
                    wait(pe, xnT_mark[b], ld["fc1"], work.free[i])
                    m = pe_p.mark(pe.matmul(bank, fc1[:, :], xnT[:, b, c * CH:(c + 1) * CH], start=True, stop=True))
                    wait(act, m, ld["fc1b"], phase_free)
                    h_mark = act_p.mark(act.activation(h1T[:, c * CH:(c + 1) * CH], bank, ACT.Identity,
                                                       bias=fc1b[:, 0:1]))
                    work.free[i] = [h_mark]
                xnT_free[b] = [m]
                for k in range(2 * KI):
                    for c in range(NC):
                        i, bank = work.take()
                        wait(pe, h_mark, ld["inp"], work.free[i])
                        m = pe_p.mark(pe.matmul(bank, inp[:, k * P:(k + 1) * P], h1T[:, c * CH:(c + 1) * CH],
                                                start=True, stop=True))
                        wait(act, m, phase_free)
                        if k < KI:
                            n = act_p.mark(act.copy(xc[:, k, PAD + c * CH:PAD + (c + 1) * CH], bank))
                            xc_mark = n
                        else:
                            n = act_p.mark(act.activation(zg[:, k - KI, c * CH:(c + 1) * CH], bank, ACT.Silu))
                            zg_mark = n
                        work.free[i] = [n]
                for k in range(KI):
                    wait(dve, xc_mark, z, ld["cw"], ld["cb"], phase_free)
                    m = dve_p.mark(dve.tensor_scalar(u[:, k, :], xc[:, k, 0:SEQ], cw[:, k, 0:1], cb[:, k:k + 1],
                                                     ALU.mult, ALU.add))
                    for w in range(1, DCONV):
                        wait(dve, m)
                        m = dve_p.mark(dve.scalar_tensor_tensor(
                            out=u[:, k, :], in0=xc[:, k, w:w + SEQ], scalar=cw[:, k, w:w + 1], in1=u[:, k, :],
                            op0=ALU.mult, op1=ALU.add))
                    wait(act, m)
                    u_mark = act_p.mark(act.activation(u[:, k, :], u[:, k, :], ACT.Silu))
                for c in range(NC):
                    i, bank = work.take()
                    cs = slice(c * CH, (c + 1) * CH)
                    wait(pe, u_mark, ld["xpj"], work.free[i])
                    for k in range(KI):
                        ins = pe.matmul(bank, xpj[:, k, :], u[:, k, cs], start=(k == 0), stop=(k == KI - 1))
                    m = pe_p.mark(ins)
                    wait(act, m, phase_free)
                    n = act_p.mark(act.copy(xdr[:, cs], bank))
                    xd_mark = act_p.mark(act.copy(xd[:, cs], bank))
                    wait(dve, m, xd_mark)
                    xdr_mark = dve_p.mark(dve.tensor_tensor(xdr[HS:P, cs], bank[HS:P, :], xdr[HS:P, cs],
                                                            ALU.subtract))
                    work.free[i] = [xd_mark, xdr_mark]
                for k in range(KI):
                    for c in range(NC):
                        i, bank = work.take()
                        cs = slice(c * CH, (c + 1) * CH)
                        wait(pe, xd_mark, ld["dtp"], work.free[i])
                        m = pe_p.mark(pe.matmul(bank, dtp[:, k * P:(k + 1) * P], xd[:, cs], start=True, stop=True))
                        wait(act, m, ld["dtb"], phase_free)
                        n = act_p.mark(act.activation(dt[:, k, cs], bank, ACT.Identity, bias=dtb[:, k:k + 1]))
                        work.free[i] = [n]
                for k in range(KI):
                    wait(act, n)
                    if k:
                        wait(act, sp_mark)
                    m = act_p.mark(act.activation(tmp1[:, :], dt[:, k, :], ACT.Abs))
                    wait(act, m)
                    m = act_p.mark(act.activation(tmp1[:, :], tmp1[:, :], ACT.Exp, scale=-1.0))
                    wait(act, m)
                    m = act_p.mark(act.activation(tmp1[:, :], tmp1[:, :], ACT.Ln, bias=1.0))
                    wait(dve, m)
                    sp_mark = dve_p.mark(dve.scalar_tensor_tensor(
                        out=dt[:, k, :], in0=dt[:, k, :], scalar=0.0, in1=tmp1[:, :], op0=ALU.max, op1=ALU.add))
                    wait(dve, sp_mark, u_mark)
                    du_mark = dve_p.mark(dve.tensor_tensor(du[:, k, :], dt[:, k, :], u[:, k, :], ALU.mult))
                Y = [banks(4, 2), banks(6, 2)]
                for n in range(NS):
                    bi, bbank = bb.take()
                    wait(pe, xdr_mark, xd_mark, pick_mark, bb.free[bi])
                    for c in range(NC):
                        ins = pe.matmul(bbank[:, c * CH:(c + 1) * CH], pickr[:, n, :], xdr[:, c * CH:(c + 1) * CH],
                                        start=True, stop=True)
                    b_mark = pe_p.mark(ins)
                    ci, call = cc.take()
                    for c in range(NC):
                        i, bank = work.take()
                        wait(pe, work.free[i])
                        m = pe_p.mark(pe.matmul(bank, pickr[:, NS + n, :], xdr[:, c * CH:(c + 1) * CH],
                                                start=True, stop=True))
                        wait(act, m, cc.free[ci])
                        c_mark = act_p.mark(act.copy(call[:, c * CH:(c + 1) * CH], bank))
                        work.free[i] = [c_mark]
                    cc.free[ci] = []
                    for k in range(KI):
                        ai, decay = dA.take()
                        wait(act, sp_mark, A_mark, dA.free[ai])
                        a_mark = act_p.mark(act.activation(decay[:, :], dt[:, k, :], ACT.Exp,
                                                           scale=alog[:, k, n:n + 1]))
                        gi, gain = dBu.take()
                        wait(dve, b_mark, du_mark, dBu.free[gi])
                        g_mark = dve_p.mark(dve.tensor_tensor(gain[:, :], bbank, du[:, k, :], ALU.mult))
                        bb.free[bi] = [g_mark]
                        si, state = hs.take()
                        wait(dve, g_mark, a_mark, hs.free[si])
                        s_mark = dve_p.mark(dve.tensor_tensor_scan(state[:, :], decay[:, :], gain[:, :], 0.0,
                                                                   ALU.mult, ALU.add))
                        dA.free[ai], dBu.free[gi] = [s_mark], [s_mark]
                        oi, hcn = hc.take()
                        wait(pool, s_mark, c_mark, hc.free[oi])
                        pool_alone()
                        o_mark = pool_p.mark(pool.tensor_tensor(hcn[:, :], state[:, :], call[:, :], ALU.mult))
                        hs.free[si] = [o_mark]
                        cc.free[ci].append(o_mark)
                        wait(pe, o_mark, phase_free)
                        for c in range(NC):
                            ins = pe.matmul(Y[k][:, c * CH:(c + 1) * CH], ident[:, :], hcn[:, c * CH:(c + 1) * CH],
                                            start=(n == 0), stop=(n == NS - 1))
                        y_mark = pe_p.mark(ins)
                        hc.free[oi] = [y_mark]
                for k in range(KI):
                    wait(dve, y_mark, ld["dsk"], zg_mark)
                    m = dve_p.mark(dve.scalar_tensor_tensor(out=du[:, k, :], in0=u[:, k, :], scalar=dsk[:, k:k + 1],
                                                            in1=Y[k], op0=ALU.mult, op1=ALU.add))
                    wait(dve, m)
                    g_mark = dve_p.mark(dve.tensor_tensor(du[:, k, :], du[:, k, :], zg[:, k, :], ALU.mult))
                for c in range(NC):
                    i, bank = work.take()
                    cs = slice(c * CH, (c + 1) * CH)
                    wait(pe, g_mark, ld["outp"], work.free[i])
                    for k in range(KI):
                        ins = pe.matmul(bank, outp[:, k, :], du[:, k, cs], start=(k == 0), stop=(k == KI - 1))
                    m = pe_p.mark(ins)
                    wait(act, m)
                    m = act_p.mark(act.copy(h1T[:, cs], bank))
                    work.free[i] = [m]
                    xs = x[:, b * NT + 4 * c:b * NT + 4 * c + 4, :]
                    wait(dve, ld["fc2b"])
                    n = dve_p.mark(dve.tensor_tensor(xs, xs, fc2b[:, :].unsqueeze(1).broadcast_to([P, 4, D]), ALU.add))
                    i, bank = work.take()
                    wait(pe, m, ld["fc2"], work.free[i])
                    for t in range(4):
                        tt = 4 * c + t
                        ins = pe.matmul(bank[:, t * P:(t + 1) * P], h1T[:, tt * P:(tt + 1) * P], fc2[:, :],
                                        start=True, stop=True)
                    m = pe_p.mark(ins)
                    wait(dve, m, n)
                    x_mark[b] = dve_p.mark(dve.tensor_tensor(xs, tile_bank(bank), xs, ALU.add))
                    work.free[i] = [x_mark[b]]
                phase_free = [m, x_mark[b]]

            for b in range(B):
                selective_scan(b)
        barrier()

        with ExitStack() as scope:
            def sba(name, shape, dt=F32):
                return sb(name, shape, dt, scope)

            w1, w2 = sba("e1_w1", [P, E1, F1]), sba("e1_w2", [P, M1, D])
            b1, b2 = sba("e1_b1", [P, M1]), sba("e1_b2", [P, D])
            all1 = sba("e1_ones", [P, P])
            gw, gb, rms = sba("e1_gw", [P, E1]), sba("e1_gb", [P, E1]), sba("e1_rms", [P, E1])
            lg, sq = sba("e1_lg", [P, NT, E1]), sba("e1_sq", [P, NT, E1])
            s1, s2 = sba("e1_s1", [P, NT]), sba("e1_s2", [P, NT])
            hT = Ring([sba(f"e1_h{i}", [P, M1, CH]) for i in range(2)])
            z = pool_set(b2[:, :], 0.0)
            z1 = pool_set(all1[:, :], 1.0)
            ld_g = [load("e1_gw", gw[:, :], a["e1_gw"]), load("e1_gb", gb[:, :], a["e1_gb"].partition_broadcast(P)),
                    load("e1_rms", rms[:, :], a["e1_rms"].partition_broadcast(P))]
            ld_w1 = [load("e1_w1", w1[:, :, :], a["e1_w1"].rearrange("e d f -> d e f")),
                     load("e1_b1", b1[:, :], a["e1_b1"])]
            ld_w2 = [load("e1_w2", w2[:, :, :], a["e1_w2"].rearrange("e (m p) d -> p (e m) d", p=P))]
            wait(sp, z)
            ld_w2.append(load("e1_b2", b2[0:E1, :], a["e1_b2"]))
            gate_free = []

            def wide(v):
                return v[:, :].unsqueeze(2).broadcast_to([P, NT, E1])

            def row(v):
                return v[:, :].unsqueeze(1).broadcast_to([P, NT, E1])

            def experts1(b):
                nonlocal gate_free
                layer_norm(b)
                i, bank = work.take()
                wait(pe, xnT_mark[b], ld_g, work.free[i])
                for t in range(NT):
                    ins = pe.matmul(bank[:, t * E1:(t + 1) * E1], xnT[:, b, t * P:(t + 1) * P], gw[:, :],
                                    start=True, stop=True)
                m = pe_p.mark(ins)
                wait(dve, m, ld_g, gate_free)
                m = dve_p.mark(dve.tensor_tensor(lg[:, :, :], bank[:, 0:NT * E1].rearrange("p (t e) -> p t e", e=E1),
                                                 row(gb), ALU.add))
                work.free[i] = [m]
                wait(dve, m)
                m = dve_p.mark(dve.tensor_tensor(sq[:, :, :], lg[:, :, :], lg[:, :, :], ALU.mult))
                wait(dve, m)
                m = dve_p.mark(dve.tensor_reduce(s1[:, :], sq[:, :, :], AXX, ALU.add))
                wait(dve, m)
                m = dve_p.mark(dve.tensor_scalar(s1[:, :], s1[:, :], 1.0 / E1, F32_EPS, ALU.mult, ALU.add))
                wait(act, m)
                m = act_p.mark(act.activation(s1[:, :], s1[:, :], ACT.Sqrt))
                wait(dve, m)
                m = dve_p.mark(dve.reciprocal(s1[:, :], s1[:, :]))
                wait(dve, m)
                m = dve_p.mark(dve.tensor_tensor(lg[:, :, :], lg[:, :, :], wide(s1), ALU.mult))
                wait(dve, m)
                m = dve_p.mark(dve.tensor_tensor(lg[:, :, :], lg[:, :, :], row(rms), ALU.mult))
                wait(dve, m)
                m = dve_p.mark(dve.tensor_reduce(s2[:, :], lg[:, :, :], AXX, ALU.max))
                wait(dve, m)
                m = dve_p.mark(dve.tensor_tensor(lg[:, :, :], lg[:, :, :], wide(s2), ALU.subtract))
                wait(act, m)
                m = act_p.mark(act.activation(lg[:, :, :], lg[:, :, :], ACT.Exp, scale=2.0))
                wait(dve, m)
                m = dve_p.mark(dve.tensor_reduce(s1[:, :], lg[:, :, :], AXX, ALU.add))
                wait(dve, m)
                m = dve_p.mark(dve.reciprocal(s1[:, :], s1[:, :]))
                wait(dve, m)
                m = dve_p.mark(dve.tensor_scalar(s2[:, :], s1[:, :], GATE_EPS, None, ALU.add))
                wait(dve, m)
                m = dve_p.mark(dve.reciprocal(s2[:, :], s2[:, :]))
                wait(dve, m)
                norm_mark = dve_p.mark(dve.tensor_tensor(s2[:, :], s2[:, :], s1[:, :], ALU.mult))

                def hidden(c):
                    k, h = hT.take()
                    for m_ in range(M1):
                        i, bank = hid.take()
                        e, f = divmod(m_, F1 // P)
                        wait(pe, ld_w1, hid.free[i])
                        m = pe_p.mark(pe.matmul(bank, w1[:, e, f * P:(f + 1) * P], xnT[:, b, c * CH:(c + 1) * CH],
                                                start=True, stop=True))
                        wait(act, m, ld_w1, hT.free[k])
                        g = act_p.mark(act.activation(h[:, m_, :], bank, ACT.Gelu, bias=b1[:, m_:m_ + 1]))
                        hid.free[i] = [g]
                    return k, h, g

                def down(c, k, h, g):
                    i, bank = ybank.take()
                    wait(pe, g, ld_w2, z1, ybank.free[i])
                    for t in range(4):
                        for m_ in range(M1):
                            pe.matmul(bank[:, t * P:(t + 1) * P], h[:, m_, t * P:(t + 1) * P], w2[:, m_, :],
                                      start=(m_ == 0), stop=False)
                        ins = pe.matmul(bank[:, t * P:(t + 1) * P], all1[:, :], b2[:, :], start=False, stop=True)
                    m = pe_p.mark(ins)
                    hT.free[k] = [m]
                    for t in range(4):
                        tt = 4 * c + t
                        xs = x[:, b * NT + tt, :]
                        wait(dve, m, norm_mark)
                        r = dve_p.mark(dve.scalar_tensor_tensor(
                            out=xs, in0=bank[:, t * P:(t + 1) * P], scalar=s2[:, tt:tt + 1],
                            in1=xs, op0=ALU.mult, op1=ALU.add))
                    ybank.free[i] = [r]
                    wait(sp, r)
                    stores.append(progress(f"st{b}{c}", 16).mark(sp.dma_start(
                        out_d[:, b * NT + 4 * c:b * NT + 4 * c + 4, :], x[:, b * NT + 4 * c:b * NT + 4 * c + 4, :])))
                    return r

                held = [(c, *hidden(c)) for c in range(NC)]
                for h in held:
                    r = down(*h)
                gate_free = [r]

            stores = []
            for b in range(B):
                experts1(b)
            wait(sp, stores)


def dve_mark_of(marks, b, dve_p):
    return (dve_p, dve_p.count)



def _layout(i):
    f = {k: np.asarray(v) for k, v in i.items()}
    A, G, S, M = "L0_attn_", "L0_ffn_", "L1_attn_", "L1_ffn_"
    heads = lambda w: w.transpose(2, 0, 1).reshape(D, H * DH)
    cols = lambda v, k: v.reshape(k, P).T
    o = {
        "x": f[A + "x"].reshape(B * SEQ, D),
        "ident": np.eye(P, dtype=np.float32),
        "wq": heads(f[A + "W_Q"]), "wk": heads(f[A + "W_K"]), "wv": heads(f[A + "W_V"]),
        "bq": np.concatenate([f[A + "b_Q"].T] * 2), "bk": np.concatenate([f[A + "b_K"].T] * 2),
        "bv": f[A + "b_V"].reshape(H * DH),
        "wo": f[A + "W_O"].transpose(0, 2, 1).reshape(NPAIR, P, D).transpose(1, 0, 2).reshape(P, NPAIR * D),
        "bo": f[A + "b_O"],
        "rank": np.arange(E0, 0, -1, dtype=np.float32),
        "e0_wg": f[G + "wg"], "e0_w1": f[G + "w1"], "e0_w2": f[G + "w2"], "e0_b2": f[G + "b2"],
        "e0_b1": cols(f[G + "b1"], E0 * M0),
        "fc1": f[S + "fc1_w"].T, "fc1b": f[S + "fc1_b"].reshape(P, 1), "inp": f[S + "in_proj_w"].T,
        "cw": f[S + "conv_w"].reshape(KI, P, DCONV).transpose(1, 0, 2), "cb": cols(f[S + "conv_b"], KI),
        "dtb": cols(f[S + "dt_proj_b"], KI),
        "alog": f[S + "A_log"].reshape(KI, P, NS).transpose(1, 0, 2), "dsk": cols(f[S + "D"], KI),
        "outp": f[S + "out_proj_w"].T.reshape(KI, P, D).transpose(1, 0, 2),
        "fc2": f[S + "fc2_w"].T, "fc2b": f[S + "fc2_b"],
        "e1_gw": f[M + "gate_w"].T, "e1_gb": f[M + "gate_b"], "e1_rms": f[M + "rms_w"],
        "e1_w1": f[M + "w1"], "e1_b1": cols(f[M + "b1"], M1), "e1_w2": f[M + "w2"], "e1_b2": f[M + "b2"],
    }
    sel = np.zeros((P, NT, P), np.float32)
    for t in range(NT):
        sel[t, t, :LO] = 1.0
        sel[NT + t, t, LO:] = 1.0
    o["sel"] = sel
    wred = np.zeros((P, P), np.float32)
    wred[:, :GATE] = f[G + "wg_red"].T
    o["e0_wred"] = wred
    rows = DTR + 2 * NS
    xpj = np.zeros((P, KI, P), np.float32)
    xw = f[S + "x_proj_w"].T.reshape(KI, P, rows).transpose(1, 0, 2)
    xpj[:, :, :rows] = xw
    xpj[:, :, 64:64 + rows] = xw
    o["xpj"] = xpj
    dtp = np.zeros((P, DI), np.float32)
    dtp[:DTR] = f[S + "dt_proj_w"].T
    o["dtp"] = dtp
    pick = np.zeros((P, 2 * NS, P), np.float32)
    for n in range(2 * NS):
        pick[DTR + n, n, :] = 1.0
        pick[64 + DTR + n, n, :] = 1.0
    o["pick"] = pick
    return {k: np.ascontiguousarray(v) for k, v in o.items()}


def kernel(**inputs):
    from concourse import bacc
    from concourse.bass_utils import run_bass_kernel_spmd

    arrays = _layout(inputs)
    nc = bacc.Bacc("TRN2", target_bir_lowering=False, num_devices=1)
    ins = {k: nc.dram_tensor("in_" + k, v.shape, mybir.dt.from_np(v.dtype), kind="ExternalInput").ap()
           for k, v in arrays.items()}
    out = nc.dram_tensor("out_x", (B * SEQ, D), F32, kind="ExternalOutput").ap()
    two_layer_program(nc, ins, out)
    r = run_bass_kernel_spmd(nc, [{"in_" + k: v for k, v in arrays.items()}], core_ids=[0])
    return r.results[0]["out_x"].reshape(B, SEQ, D)
```

```python
from contextlib import ExitStack

import numpy as np

import concourse.bass as bass
from concourse import mybir

F32 = mybir.dt.float32
F32R = mybir.dt.float32r
ACT = mybir.ActivationFunctionType
ALU = mybir.AluOpType
AXX = mybir.AxisListType.X

P = 128
B, SEQ, D = 2, 1024, 128
NT = SEQ // P
CH = 512
NC = SEQ // CH
H, DH = 16, 64
NPAIR = H // 2
E0, F0, GATE = 8, 512, 16
M0 = F0 // P
DI, NS, DTR, DCONV = 256, 16, 8, 4
KI = DI // P
E1, F1 = 8, 256
M1 = E1 * F1 // P
LO = 64
LN_EPS, NORM_EPS, GATE_EPS = 1e-5, 1e-4, 1e-6
F32_EPS = float(np.finfo(np.float32).eps)


class Progress:

    def __init__(self, sem, step=1):
        self.sem, self.step, self.count = sem, step, 0

    def mark(self, instruction):
        instruction.then_inc(self.sem, self.step)
        self.count += self.step
        return (self, self.count)


class Waits:

    def __init__(self):
        self.seen = {}

    def __call__(self, engine, *marks):
        for m in marks:
            if m is None:
                continue
            if isinstance(m, list):
                self(engine, *m)
                continue
            progress, level = m
            key = (id(engine), progress)
            if self.seen.get(key, 0) < level:
                engine.wait_ge(progress.sem, level)
                self.seen[key] = level


class Ring:

    def __init__(self, buffers):
        self.buffers, self.free, self.at = buffers, [[] for _ in buffers], -1

    def take(self):
        self.at = (self.at + 1) % len(self.buffers)
        return self.at, self.buffers[self.at]


def two_layer_program(nc, a, out):
    pe, act, dve, pool, sp = nc.tensor, nc.scalar, nc.vector, nc.gpsimd, nc.sync
    wait = Waits()
    with ExitStack() as ctx:
        def sb(name, shape, dt=F32, scope=ctx):
            return scope.enter_context(nc.sbuf_tensor(name, shape, dt))

        def progress(name, step=1):
            return Progress(ctx.enter_context(nc.semaphore(name)), step)

        pe_p, act_p, dve_p, pool_p = (progress(n) for n in ("pe_done", "act_done", "dve_done", "pool_done"))

        def pool_alone():
            wait(pool, (pool_p, pool_p.count))

        def pool_set(dst, value):
            pool_alone()
            return pool_p.mark(pool.memset(dst, value))

        psum = ctx.enter_context(nc.psum_tensor("psum", [P, 8 * CH], F32))

        def banks(first, n=1):
            return psum[:, first * CH:(first + n) * CH]

        work = Ring([banks(0), banks(1)])

        def load(name, dst, src):
            return progress("ld_" + name, 16).mark(sp.dma_start(dst, src))

        x = sb("x", [P, B * NT, D])
        xnT = sb("xnT", [P, B, SEQ])
        ident = sb("ident", [P, P])
        xn = sb("xn", [P, NT, D])
        stats = sb("stats", [P, NT, 6])
        mv = sb("mv", [P, NT, 2])
        rstd = sb("rstd", [P, NT])
        std = sb("std", [P, NT])
        x_d = a["x"].rearrange("(t p) d -> p t d", p=P)
        out_d = out.rearrange("(t p) d -> p t d", p=P)
        ld_x = [load(f"x{b}", x[:, b * NT:(b + 1) * NT, :], x_d[:, b * NT:(b + 1) * NT, :]) for b in range(B)]
        ld_ident = load("ident", ident[:, :], a["ident"])
        x_mark = list(ld_x)
        xnT_mark = [[], []]
        xnT_free = [[], []]
        ln_free = []

        def layer_norm(b):
            nonlocal ln_free
            wait(dve, x_mark[b], *ln_free)
            for t in range(NT):
                m = dve_p.mark(dve.bn_stats(stats[:, t, :], x[:, b * NT + t, :]))
            wait(dve, m)
            for t in range(NT):
                m = dve_p.mark(dve.bn_aggr(mv[:, t, :], stats[:, t, :]))
            wait(dve, m)
            m = dve_p.mark(dve.tensor_scalar(std[:, :], mv[:, :, 1], LN_EPS, None, ALU.add))
            wait(act, m)
            m = act_p.mark(act.activation(std[:, :], std[:, :], ACT.Sqrt))
            wait(dve, m)
            m = dve_p.mark(dve.reciprocal(rstd[:, :], std[:, :]))
            wait(dve, m)
            rows = []
            for t in range(NT):
                rows.append(dve_p.mark(dve.tensor_scalar(
                    xn[:, t, :], x[:, b * NT + t, :], mv[:, t, 0:1], rstd[:, t:t + 1], ALU.subtract, ALU.mult)))
            ends = []
            for g in range(NT // 4):
                i, bank = work.take()
                wait(pe, rows[4 * g + 3], ld_ident, *work.free[i])
                for t in range(4):
                    ins = pe.transpose(bank[:, t * P:(t + 1) * P], xn[:, 4 * g + t, :], ident[:, :])
                m = pe_p.mark(ins)
                wait(act, m, *xnT_free[b])
                ends.append(act_p.mark(act.copy(xnT[:, b, g * CH:(g + 1) * CH], bank)))
                work.free[i] = [ends[-1]]
            ln_free = [m]
            xnT_mark[b] = [ends[-1]]
            xnT_free[b] = []

        with ExitStack() as scope:
            def sba(name, shape, dt=F32):
                return sb(name, shape, dt, scope)

            wq, wk, wv, wo = (sba(n, [P, H * DH]) for n in ("wq", "wk", "wv", "wo"))
            bq, bk = sba("bq", [P, NPAIR]), sba("bk", [P, NPAIR])
            bv, bo = sba("bv", [P, H * DH]), sba("bo", [P, D])
            ones = sba("ones", [P, 1])
            sel = sba("sel", [P, NT, P])
            V = sba("V", [P, NT, H * DH])
            K1, K2, Q1, Q2 = ([[sba(f"{n}{q}{s}", [P, SEQ], F32R) for s in range(2)] for q in range(2)]
                              for n in ("K1_", "K2_", "Q1_", "Q2_"))
            NPB = 3
            prob = [Ring([sba(f"prob{s}{i}", [P, SEQ]) for i in range(NPB)]) for s in range(2)]
            psums = [[sba(f"psums{q}{s}", [P, SEQ]) for s in range(2)] for q in range(2)]
            mx = sba("mx", [P, 2, NT, NC])
            nmx = [sba(f"nmx{s}", [P, P]) for s in range(2)]
            mrow = [sba(f"mrow{s}", [P, P], F32R) for s in range(2)]
            rs = sba("rs", [P, P])
            rsT = sba("rsT", [P, P])
            oraw = sba("oraw", [P, SEQ])
            onorm = sba("onorm", [P, SEQ])

            ld_wk = load("wk", wk[:, :], a["wk"])
            ld_wq = load("wq", wq[:, :], a["wq"])
            ld_b = [load("bk", bk[:, :], a["bk"]), load("bq", bq[:, :], a["bq"])]
            ld_wv = [load("wv", wv[:, :], a["wv"]), load("bv", bv[:, :], a["bv"].partition_broadcast(P))]
            ld_wo = [load("wo", wo[:, :], a["wo"]), load("bo", bo[:, :], a["bo"].partition_broadcast(P))]
            ld_sel = load("sel", sel[:, :, :], a["sel"])

            HALF = [slice(0, LO), slice(LO, P)]
            REST = [slice(LO, P), slice(0, LO)]
            GROW = [slice(LO, LO + 1), slice(0, 1)]
            for q in range(2):
                for s in range(2):
                    pool_set(Q2[q][s][REST[s], :].bitcast(F32), 0.0)
                    pool_set(K2[q][s][REST[s], :].bitcast(F32), 0.0)
            pool_set(ones[:, :], 1.0)
            for z in (nmx[0], nmx[1], rs):
                pool_set(z[:, :], 0.0)
            for q in range(2):
                for s in range(2):
                    init = pool_set(K2[q][s][GROW[s], :].bitcast(F32), 1.0)

            guard = [[progress(f"guard{q}{s}", 16) for s in range(2)] for q in range(2)]
            guard_mark = [[None, None], [None, None]]
            qk_mark = [[{}, {}], [{}, {}]]
            score_mark = [[], []]
            S = [banks(2, 2), banks(4, 2)]
            S_free = [[], []]
            O = banks(6, 2)
            O_free = []
            oraw_free, onorm_free, rsT_free, rs_free = [], [], [], []
            mx_free, nmx_free, mrow_free = [[], []], [[], []], [[], []]
            psums_mark, psums_free = [[None, None], [None, None]], [[], []]
            prob_mark = {}
            pv_end = {}
            V_mark = [None] * NT
            pv_mark = [None] * NT

            def values(b, t):
                for c in range(2):
                    i, bank = work.take()
                    wait(pe, xnT_mark[b], ld_wv, work.free[i])
                    m = pe_p.mark(pe.matmul(bank, xnT[:, b, t * P:(t + 1) * P], wv[:, c * CH:(c + 1) * CH],
                                            start=True, stop=True))
                    wait(dve, m, ld_wv, pv_mark[t])
                    V_mark[t] = dve_p.mark(dve.tensor_tensor(V[:, t, c * CH:(c + 1) * CH], bank,
                                                             bv[:, c * CH:(c + 1) * CH], ALU.add))
                    work.free[i] = [V_mark[t]]

            def project(pair, kind, c):
                b, p = divmod(pair, NPAIR)
                q = pair % 2
                w, bias, full, part = (wk, bk, K1, K2) if kind == "k" else (wq, bq, Q1, Q2)
                cs = slice(c * CH, (c + 1) * CH)
                i, bank = work.take()
                wait(pe, xnT_mark[b], ld_wk, ld_wq, work.free[i])
                m = pe_p.mark(pe.matmul(bank, w[:, 2 * p * DH:(2 * p + 2) * DH], xnT[:, b, cs], start=True, stop=True))
                wait(act, m, ld_b, score_mark[q])
                hi = [act_p.mark(act.activation(full[q][s][HALF[s], cs], bank[HALF[s], :], ACT.Identity,
                                                bias=bias[HALF[s], p:p + 1])) for s in range(2)]
                wait(dve, m, ld_b, score_mark[q], init)
                for s in range(2):
                    wait(dve, hi)
                    lo = full[q][s][REST[s], cs] if kind == "k" else part[q][s][HALF[s], cs]
                    m = dve_p.mark(dve.scalar_tensor_tensor(
                        out=lo, in0=bank[HALF[s], :], scalar=bias[HALF[s], p:p + 1],
                        in1=full[q][s][HALF[s], cs], op0=ALU.add, op1=ALU.subtract))
                    copy = part[q][s][HALF[s], cs] if kind == "k" else full[q][s][REST[s], cs]
                    n = dve_p.mark(dve.tensor_copy(copy, full[q][s][HALF[s], cs]))
                    qk_mark[q][s][kind, c] = [n]
                work.free[i] = [m]

            def row_max(pair, s, t, c):
                q = pair % 2
                i, bank = work.take()
                wait(pe, qk_mark[q][s]["k", c], qk_mark[q][s]["q", t * P // CH], work.free[i])
                m = pe_p.mark(pe.matmul(bank, Q1[q][s][:, t * P:(t + 1) * P], K1[q][s][:, c * CH:(c + 1) * CH],
                                        start=True, stop=True))
                wait(dve, m, mx_free[s])
                r = dve_p.mark(dve.tensor_reduce(mx[:, s, t, c:c + 1], bank, AXX, ALU.max))
                work.free[i] = [r]
                max_mark[s] = r

            def guard_row(pair, s):
                q = pair % 2
                wait(dve, max_mark[s], nmx_free[s], init)
                m = dve_p.mark(dve.tensor_reduce(nmx[s][:, 0:NT], mx[:, s, :, :], AXX, ALU.max, negate=True))
                mx_free[s] = [m]
                i, bank = work.take()
                wait(pe, m, ld_ident, work.free[i])
                m = pe_p.mark(pe.transpose(bank[:, 0:P], nmx[s][:, :], ident[:, :]))
                nmx_free[s] = [m]
                wait(dve, m, mrow_free[s])
                m = dve_p.mark(dve.tensor_copy(mrow[s][0:NT, :], bank[0:NT, 0:P]))
                work.free[i] = [m]
                wait(sp, m, score_mark[q], init)
                guard_mark[q][s] = guard[q][s].mark(sp.dma_start(
                    Q2[q][s][GROW[s], :].rearrange("o (t k) -> o t k", t=NT).bitcast(F32),
                    mrow[s][0:NT, :].bitcast(F32)))
                mrow_free[s] = [guard_mark[q][s]]

            def scores_hi(pair, j, s):
                q = pair % 2
                wait(pe, list(qk_mark[q][s].values()), S_free[s])
                for c in range(NC):
                    pe.matmul(S[s][:, c * CH:(c + 1) * CH], K1[q][s][:, j * P:(j + 1) * P],
                              Q1[q][s][:, c * CH:(c + 1) * CH], start=True, stop=False)

            def scores_lo(pair, j, s):
                q = pair % 2
                wait(pe, guard_mark[q][s], init)
                for c in range(NC):
                    ins = pe.matmul(S[s][:, c * CH:(c + 1) * CH], K2[q][s][:, j * P:(j + 1) * P],
                                    Q2[q][s][:, c * CH:(c + 1) * CH], start=False, stop=True)
                m = pe_p.mark(ins)
                score_mark[q] = [m]
                i, weights = prob[s].take()
                wait(act, m, prob[s].free[i])
                e = act_p.mark(act.activation(weights[:, :], S[s], ACT.Exp, scale=float(DH) ** -0.5))
                S_free[s] = [e]
                prob_mark[pair, j, s] = (i, e)
                if j == 0:
                    return
                total = psums[q][s]
                before = prob[s].buffers[prob_mark[pair, 0, s][0]] if j == 1 else total
                wait(pool, e, prob_mark[pair, 0, s][1], psums_free[q], psums_mark[q][s])
                pool_alone()
                psums_mark[q][s] = pool_p.mark(pool.tensor_tensor(total[:, :], before[:, :], weights[:, :], ALU.add))
                if j == 1:
                    prob[s].free[prob_mark[pair, 0, s][0]].append(psums_mark[q][s])
                prob[s].free[i] = [psums_mark[q][s]]

            def weighted_values(pair, j, c):
                p = pair % NPAIR
                slots = [prob_mark[pair, j, s] for s in range(2)]
                wait(pe, V_mark[j], *(e for _, e in slots))
                if j == 0:
                    wait(pe, O_free)
                for s in range(2):
                    h = 2 * p + s
                    ins = pe.matmul(O[s * LO:(s + 1) * LO, c * CH:(c + 1) * CH], V[:, j, h * DH:(h + 1) * DH],
                                    prob[s].buffers[slots[s][0]][:, c * CH:(c + 1) * CH],
                                    start=(j == 0), stop=(j == NT - 1))
                if c == NC - 1:
                    m = pv_mark[j] = pe_p.mark(ins)
                    for s in range(2):
                        prob[s].free[slots[s][0]] = prob[s].free[slots[s][0]] + [m]
                    if j == NT - 1:
                        pv_end[pair] = m

            def take_out(pair):
                nonlocal O_free
                wait(act, pv_end[pair], oraw_free)
                O_free = [act_p.mark(act.copy(oraw[:, :], O))]

            max_mark = [None, None]
            onorm_mark = None
            rsT_mark = [None, None]

            def inverse_sums(pair):
                q = pair % 2
                i, bank = work.take()
                wait(pe, psums_mark[q], work.free[i], init)
                for s in range(2):
                    for t in range(NT):
                        ins = pe.matmul(bank[:, s * NT + t:s * NT + t + 1], psums[q][s][:, t * P:(t + 1) * P],
                                        ones[:, :], start=True, stop=True)
                m = pe_p.mark(ins)
                psums_free[q] = [m]
                wait(dve, m, rs_free, init)
                rsT_mark[0] = dve_p.mark(dve.reciprocal(rs[:, 0:2 * NT], bank[:, 0:2 * NT]))
                work.free[i] = [rsT_mark[0]]

            def turn_sums(pair):
                nonlocal rs_free
                i, bank = work.take()
                wait(pe, rsT_mark[0], ld_ident, work.free[i])
                m = pe_p.mark(pe.transpose(bank[:, 0:P], rs[:, :], ident[:, :]))
                rs_free = [m]
                wait(dve, m, rsT_free)
                rsT_mark[1] = dve_p.mark(dve.tensor_copy(rsT[:, :], bank[:, 0:P]))
                work.free[i] = [rsT_mark[1]]

            def normalise(pair, c):
                nonlocal rsT_free, oraw_free, onorm_mark
                i, bank = work.take()
                wait(pe, rsT_mark[1], ld_sel, work.free[i])
                for t in range(4):
                    ins = pe.matmul(bank[:, t * P:(t + 1) * P], sel[:, 4 * c + t, :], rsT[:, :], start=True, stop=True)
                m = pe_p.mark(ins)
                wait(dve, m, O_free, onorm_free)
                onorm_mark = dve_p.mark(dve.tensor_tensor(onorm[:, c * CH:(c + 1) * CH], bank,
                                                          oraw[:, c * CH:(c + 1) * CH], ALU.mult))
                work.free[i] = [onorm_mark]
                rsT_free, oraw_free = [m], [onorm_mark]

            def project_out(pair, c):
                nonlocal onorm_free
                b, p = divmod(pair, NPAIR)
                i, bank = work.take()
                wait(pe, onorm_mark, ld_wo, work.free[i])
                for t in range(4):
                    ins = pe.matmul(bank[:, t * P:(t + 1) * P], onorm[:, (4 * c + t) * P:(4 * c + t + 1) * P],
                                    wo[:, p * D:(p + 1) * D], start=True, stop=True)
                m = pe_p.mark(ins)
                wait(dve, m, x_mark[b])
                xs = x[:, b * NT + 4 * c:b * NT + 4 * c + 4, :]
                x_mark[b] = dve_p.mark(dve.tensor_tensor(xs, bank.rearrange("p (t d) -> p t d", d=D), xs, ALU.add))
                work.free[i] = [x_mark[b]]
                onorm_free = [m]

            def start_batch(b):
                layer_norm(b)
                wait(dve, ld_wo, (dve_p, dve_p.count))
                xs = x[:, b * NT:(b + 1) * NT, :]
                x_mark[b] = dve_p.mark(dve.tensor_tensor(
                    xs, xs, bo[:, :].unsqueeze(1).broadcast_to([P, NT, D]), ALU.add))

            def side_work(pair, nxt):
                early, late = [], []
                if nxt is not None:
                    early = [lambda k=k, c=c: project(nxt, k, c) for k in "kq" for c in range(NC)]
                    for s in range(2):
                        late += [lambda s=s, t=t, c=c: row_max(nxt, s, t, c)
                                 for ts in (range(NT // 2), range(NT // 2, NT)) for c in range(NC) for t in ts]
                        late.append(lambda s=s: guard_row(nxt, s))
                if pair is not None:
                    ends = [lambda: inverse_sums(pair), lambda: turn_sums(pair)]
                    ends += [lambda f=f, c=c: f(pair, c) for f in (normalise, project_out) for c in range(NC)]
                    for n, f in enumerate(ends):
                        late.insert(4 + 4 * n, f)
                return early, late

            start_batch(0)
            first = side_work(None, 0)
            for n, job in enumerate(first[0] + first[1]):
                job()
                if n % 4 == 3 and n // 4 < NT:
                    values(0, n // 4)
            npairs = B * NPAIR
            for pair in range(npairs):
                early, late = side_work(pair - 1 if pair else None, pair + 1 if pair + 1 < npairs else None)
                GAP = 3
                slots = 6 * NT
                at, nearly, nlate = 0, GAP * len(early) + 1, len(late)

                def side():
                    nonlocal at
                    if at < nearly:
                        if at % GAP == 0 and early:
                            early.pop(0)()
                    else:
                        due = nlate * (at - nearly + 1) / (slots - nearly)
                        while late and nlate - len(late) < due:
                            late.pop(0)()
                    at += 1

                for j in range(NT):
                    before = (pair, j - 1) if j else (pair - 1, NT - 1)
                    for s in range(2):
                        scores_hi(pair, j, s)
                        side()
                        scores_lo(pair, j, s)
                        side()
                        if before[0] >= 0:
                            weighted_values(*before, s)
                            if s == 1 and j == 0:
                                take_out(pair - 1)
                        side()
                    if before[0] == NPAIR - 1:
                        values(1, before[1])
                    if pair == 2 and j == 4:
                        start_batch(1)
            for c in range(NC):
                weighted_values(npairs - 1, NT - 1, c)
            take_out(npairs - 1)
            for job in side_work(npairs - 1, None)[1]:
                job()

        def barrier():
            ends = [(p, p.count) for p in (pe_p, act_p, dve_p, pool_p)]
            for engine in (pe, act, dve, pool, sp):
                wait(engine, ends)

        barrier()
        hid = Ring([banks(i) for i in range(2, 6)])
        ybank = Ring([banks(6), banks(7)])

        def tile_bank(bank):
            return bank.rearrange("p (t d) -> p t d", d=D)

        with ExitStack() as scope:
            def sba(name, shape, dt=F32):
                return sb(name, shape, dt, scope)

            w1, w2 = sba("e0_w1", [P, E0, F0]), sba("e0_w2", [P, E0, M0, D])
            b1 = sba("e0_b1", [P, E0 * M0])
            b2 = sba("e0_b2", [P, NT, D])
            wred = sba("e0_wred", [P, P])
            wg, wgsq = sba("e0_wg", [P, P]), sba("e0_wgsq", [E0, GATE])
            wgn = sba("e0_wgn", [E0, 1])
            wgu = sba("e0_wgu", [P, E0])
            rank = sba("e0_rank", [P, E0])
            xrT = sba("e0_xrT", [P, SEQ])
            lg, ex, one = (sba(f"e0_{n}", [P, NT, E0]) for n in ("logits", "exps", "onehot"))
            coef = sba("e0_coef", [P, P])
            coefT = sba("e0_coefT", [P, P])
            top, score = sba("e0_top", [P, NT]), sba("e0_score", [P, NT])
            hT = Ring([sba(f"e0_h{i}", [P, M0, CH]) for i in range(2)])

            z0 = pool_set(wg[:, :], 0.0)
            pool_set(b2[:, :, :], 0.0)
            z1 = pool_set(coef[:, :], 0.0)
            ld_g = [load("e0_wred", wred[:, :], a["e0_wred"]),
                    load("e0_rank", rank[:, :], a["rank"].partition_broadcast(P))]
            wait(sp, z0)
            ld_wg = load("e0_wg", wg[0:E0, 0:GATE], a["e0_wg"])
            ld_w1 = [load(f"e0_w1{e}", w1[:, e, :], a["e0_w1"][e]) for e in range(E0)]
            ld_w2 = [load(f"e0_w2{e}", w2[:, e, :, :], a["e0_w2"][e].rearrange("(m p) d -> p m d", p=P))
                     for e in range(E0)]
            ld_b1 = load("e0_b1", b1[:, :], a["e0_b1"])
            wait(sp, z1)
            ld_b2 = [load(f"e0_b2{t}", b2[E0 * t:E0 * (t + 1), t, :], a["e0_b2"]) for t in range(NT)]

            wait(dve, ld_wg)
            m = dve_p.mark(dve.tensor_tensor(wgsq[:, :], wg[0:E0, 0:GATE], wg[0:E0, 0:GATE], ALU.mult))
            wait(dve, m)
            m = dve_p.mark(dve.tensor_reduce(wgn[:, :], wgsq[:, :], AXX, ALU.add))
            wait(act, m)
            m = act_p.mark(act.activation(wgn[:, :], wgn[:, :], ACT.Sqrt))
            wait(dve, m)
            m = dve_p.mark(dve.tensor_scalar(wgn[:, :], wgn[:, :], NORM_EPS, None, ALU.max))
            wait(dve, m)
            m = dve_p.mark(dve.reciprocal(wgn[:, :], wgn[:, :]))
            wait(dve, m)
            m = dve_p.mark(dve.tensor_scalar(wg[0:E0, 0:GATE], wg[0:E0, 0:GATE], wgn[:, 0:1], None, ALU.mult))
            i, bank = work.take()
            wait(pe, m, z0, work.free[i])
            m = pe_p.mark(pe.transpose(bank[:, 0:P], wg[:, :], ident[:, :]))
            wait(dve, m)
            wgu_mark = dve_p.mark(dve.tensor_copy(wgu[:, :], bank[:, 0:E0]))
            work.free[i] = [wgu_mark]
            gate_free = []

            def experts0(b):
                nonlocal gate_free
                layer_norm(b)
                for c in range(NC):
                    i, bank = work.take()
                    wait(pe, xnT_mark[b], ld_g, work.free[i])
                    m = pe_p.mark(pe.matmul(bank, wred[:, :], xnT[:, b, c * CH:(c + 1) * CH], start=True, stop=True))
                    wait(act, m, gate_free)
                    m = act_p.mark(act.copy(xrT[:, c * CH:(c + 1) * CH], bank))
                    work.free[i] = [m]
                i, bank = work.take()
                wait(pe, m, wgu_mark, work.free[i])
                for t in range(NT):
                    ins = pe.matmul(bank[:, t * E0:(t + 1) * E0], xrT[:, t * P:(t + 1) * P], wgu[:, :],
                                    start=True, stop=True)
                m = pe_p.mark(ins)

                def wide(v):
                    return v[:, :].unsqueeze(2).broadcast_to([P, NT, E0])

                flat = bank[:, 0:NT * E0].rearrange("p (t e) -> p t e", e=E0)
                wait(dve, m, gate_free)
                m = dve_p.mark(dve.tensor_reduce(top[:, :], flat, AXX, ALU.max))
                wait(dve, m)
                m = dve_p.mark(dve.tensor_tensor(lg[:, :, :], flat, wide(top), ALU.subtract))
                work.free[i] = [m]
                wait(act, m)
                n = act_p.mark(act.activation(ex[:, :, :], lg[:, :, :], ACT.Exp))
                wait(dve, m, ld_g)
                m = dve_p.mark(dve.tensor_scalar(one[:, :, :], lg[:, :, :], 0.0, None, ALU.is_equal))
                wait(dve, m)
                m = dve_p.mark(dve.tensor_tensor(one[:, :, :], one[:, :, :],
                                                 rank[:, :].unsqueeze(1).broadcast_to([P, NT, E0]), ALU.mult))
                wait(dve, m)
                m = dve_p.mark(dve.tensor_reduce(top[:, :], one[:, :, :], AXX, ALU.max))
                wait(dve, m)
                m = dve_p.mark(dve.tensor_tensor(one[:, :, :], one[:, :, :], wide(top), ALU.is_equal))
                wait(dve, n)
                m = dve_p.mark(dve.tensor_reduce(score[:, :], ex[:, :, :], AXX, ALU.add))
                wait(dve, m)
                m = dve_p.mark(dve.reciprocal(score[:, :], score[:, :]))
                wait(dve, m, z1)
                cview = coef[:, 0:NT * E0].rearrange("p (t e) -> p t e", e=E0)
                coef_mark = dve_p.mark(dve.tensor_tensor(cview, one[:, :, :], wide(score), ALU.mult))
                i, bank = work.take()
                wait(pe, coef_mark, work.free[i])
                m = pe_p.mark(pe.transpose(bank[:, 0:P], coef[:, :], ident[:, :]))
                wait(dve, m)
                m = dve_p.mark(dve.tensor_copy(coefT[:, :], bank[:, 0:P]))
                work.free[i] = [m]
                for c in range(NC):
                    i, bank = work.take()
                    wait(pe, m, ld_b2, work.free[i])
                    for t in range(4):
                        ins = pe.matmul(bank[:, t * P:(t + 1) * P], coefT[:, :], b2[:, 4 * c + t, :],
                                        start=True, stop=True)
                    n = pe_p.mark(ins)
                    xs = x[:, b * NT + 4 * c:b * NT + 4 * c + 4, :]
                    wait(dve, n)
                    x_mark[b] = dve_p.mark(dve.tensor_tensor(xs, tile_bank(bank), xs, ALU.add))
                    work.free[i] = [x_mark[b]]

                def hidden(e, c):
                    k, h = hT.take()
                    for m_ in range(M0):
                        i, bank = hid.take()
                        wait(pe, ld_w1[e], hid.free[i])
                        m = pe_p.mark(pe.matmul(bank, w1[:, e, m_ * P:(m_ + 1) * P], xnT[:, b, c * CH:(c + 1) * CH],
                                                start=True, stop=True))
                        wait(act, m, ld_b1, hT.free[k])
                        g = act_p.mark(act.activation(h[:, m_, :], bank, ACT.Gelu,
                                                      bias=b1[:, e * M0 + m_:e * M0 + m_ + 1]))
                        hid.free[i] = [g]
                    xnT_free[b] = [m]
                    return k, h, g

                def down(e, c, k, h, g):
                    i, bank = ybank.take()
                    wait(pe, g, ld_w2[e], ybank.free[i])
                    for t in range(4):
                        for m_ in range(M0):
                            ins = pe.matmul(bank[:, t * P:(t + 1) * P], h[:, m_, t * P:(t + 1) * P], w2[:, e, m_, :],
                                            start=(m_ == 0), stop=(m_ == M0 - 1))
                    m = pe_p.mark(ins)
                    hT.free[k] = [m]
                    for t in range(4):
                        tt = 4 * c + t
                        xs = x[:, b * NT + tt, :]
                        wait(dve, m, x_last[tt])
                        x_last[tt] = dve_p.mark(dve.scalar_tensor_tensor(
                            out=xs, in0=bank[:, t * P:(t + 1) * P], scalar=coef[:, tt * E0 + e:tt * E0 + e + 1],
                            in1=xs, op0=ALU.mult, op1=ALU.add))
                    ybank.free[i] = [x_last[tt]]

                x_last = [x_mark[b]] * NT
                todo = [(e, c) for e in range(E0) for c in range(NC)]
                held = None
                for unit in todo:
                    new = (*unit, *hidden(*unit))
                    if held:
                        down(*held)
                    held = new
                down(*held)
                x_mark[b] = x_last[NT - 1]
                gate_free = [x_mark[b]]

            for b in range(B):
                experts0(b)
        barrier()

        with ExitStack() as scope:
            def sba(name, shape, dt=F32):
                return sb(name, shape, dt, scope)

            HS = 64
            PAD = DCONV - 1
            fc1, inp = sba("fc1", [P, D]), sba("inp", [P, 2 * DI])
            fc1b = sba("fc1b", [P, 1])
            cw, cb = sba("cw", [P, KI, DCONV]), sba("cb", [P, KI])
            xpj = sba("xpj", [P, KI, P])
            dtp, dtb = sba("dtp", [P, DI]), sba("dtb", [P, KI])
            alog, dsk = sba("alog", [P, KI, NS]), sba("dsk", [P, KI])
            outp, fc2, fc2b = sba("outp", [P, KI, D]), sba("fc2", [P, D]), sba("fc2b", [P, D])
            pick = sba("pick", [P, 2 * NS, P])
            pickr = sba("pickr", [P, 2 * NS, P], F32R)
            h1T = sba("h1T", [P, SEQ])
            xc = sba("xc", [P, KI, PAD + SEQ])
            u, dt, du, zg = (sba(n, [P, KI, SEQ]) for n in ("u", "dt", "du", "zg"))
            xd = sba("xd", [P, SEQ])
            xdr = sba("xdr", [P, SEQ], F32R)
            tmp1, tmp2 = sba("tmp1", [P, SEQ]), sba("tmp2", [P, SEQ])
            dA = Ring([sba(f"dA{i}", [P, SEQ]) for i in range(4)])
            dBu = Ring([sba(f"dBu{i}", [P, SEQ]) for i in range(2)])
            hs = Ring([sba(f"hs{i}", [P, SEQ]) for i in range(2)])
            hc = Ring([sba(f"hc{i}", [P, SEQ]) for i in range(3)])
            cc = Ring([sba(f"cc{i}", [P, SEQ]) for i in range(2)])
            bb = Ring([sba(f"bb{i}", [P, SEQ]) for i in range(2)])
            spread_bank = Ring([banks(2), banks(3)])

            z = pool_set(xc[:, :, 0:PAD], 0.0)
            ld = {}
            for name, t in (("fc1", fc1), ("fc1b", fc1b), ("inp", inp), ("cw", cw), ("cb", cb), ("xpj", xpj),
                            ("dtp", dtp), ("dtb", dtb), ("alog", alog), ("dsk", dsk), ("outp", outp), ("fc2", fc2),
                            ("pick", pick)):
                ld[name] = load("s_" + name, t[:], a[name])
            ld["fc2b"] = load("s_fc2b", fc2b[:, :], a["fc2b"].partition_broadcast(P))
            wait(dve, ld["pick"])
            pick_mark = dve_p.mark(dve.tensor_copy(pickr[:, :, :], pick[:, :, :]))
            wait(act, ld["alog"])
            A_mark = act_p.mark(act.activation(alog[:, :, :], alog[:, :, :], ACT.Exp))
            wait(dve, A_mark)
            A_mark = dve_p.mark(dve.tensor_scalar(alog[:, :, :], alog[:, :, :], -1.0, None, ALU.mult))
            phase_free = []

            def selective_scan(b):
                nonlocal phase_free
                layer_norm(b)
                for c in range(NC):
                    i, bank = work.take()
                    wait(pe, xnT_mark[b], ld["fc1"], work.free[i])
                    m = pe_p.mark(pe.matmul(bank, fc1[:, :], xnT[:, b, c * CH:(c + 1) * CH], start=True, stop=True))
                    wait(act, m, ld["fc1b"], phase_free)
                    h_mark = act_p.mark(act.activation(h1T[:, c * CH:(c + 1) * CH], bank, ACT.Identity,
                                                       bias=fc1b[:, 0:1]))
                    work.free[i] = [h_mark]
                xnT_free[b] = [m]
                for k in range(2 * KI):
                    for c in range(NC):
                        i, bank = work.take()
                        wait(pe, h_mark, ld["inp"], work.free[i])
                        m = pe_p.mark(pe.matmul(bank, inp[:, k * P:(k + 1) * P], h1T[:, c * CH:(c + 1) * CH],
                                                start=True, stop=True))
                        wait(act, m, phase_free)
                        if k < KI:
                            n = act_p.mark(act.copy(xc[:, k, PAD + c * CH:PAD + (c + 1) * CH], bank))
                            xc_mark = n
                        else:
                            n = act_p.mark(act.activation(zg[:, k - KI, c * CH:(c + 1) * CH], bank, ACT.Silu))
                            zg_mark = n
                        work.free[i] = [n]
                for k in range(KI):
                    wait(dve, xc_mark, z, ld["cw"], ld["cb"], phase_free)
                    m = dve_p.mark(dve.tensor_scalar(u[:, k, :], xc[:, k, 0:SEQ], cw[:, k, 0:1], cb[:, k:k + 1],
                                                     ALU.mult, ALU.add))
                    for w in range(1, DCONV):
                        wait(dve, m)
                        m = dve_p.mark(dve.scalar_tensor_tensor(
                            out=u[:, k, :], in0=xc[:, k, w:w + SEQ], scalar=cw[:, k, w:w + 1], in1=u[:, k, :],
                            op0=ALU.mult, op1=ALU.add))
                    wait(act, m)
                    u_mark = act_p.mark(act.activation(u[:, k, :], u[:, k, :], ACT.Silu))
                for c in range(NC):
                    i, bank = work.take()
                    cs = slice(c * CH, (c + 1) * CH)
                    wait(pe, u_mark, ld["xpj"], work.free[i])
                    for k in range(KI):
                        ins = pe.matmul(bank, xpj[:, k, :], u[:, k, cs], start=(k == 0), stop=(k == KI - 1))
                    m = pe_p.mark(ins)
                    wait(act, m, phase_free)
                    n = act_p.mark(act.copy(xdr[:, cs], bank))
                    xd_mark = act_p.mark(act.copy(xd[:, cs], bank))
                    wait(dve, m, xd_mark)
                    xdr_mark = dve_p.mark(dve.tensor_tensor(xdr[HS:P, cs], bank[HS:P, :], xdr[HS:P, cs],
                                                            ALU.subtract))
                    work.free[i] = [xd_mark, xdr_mark]
                for k in range(KI):
                    for c in range(NC):
                        i, bank = work.take()
                        cs = slice(c * CH, (c + 1) * CH)
                        wait(pe, xd_mark, ld["dtp"], work.free[i])
                        m = pe_p.mark(pe.matmul(bank, dtp[:, k * P:(k + 1) * P], xd[:, cs], start=True, stop=True))
                        wait(act, m, ld["dtb"], phase_free)
                        n = act_p.mark(act.activation(dt[:, k, cs], bank, ACT.Identity, bias=dtb[:, k:k + 1]))
                        work.free[i] = [n]
                for k in range(KI):
                    wait(act, n)
                    if k:
                        wait(act, sp_mark)
                    m = act_p.mark(act.activation(tmp1[:, :], dt[:, k, :], ACT.Abs))
                    wait(act, m)
                    m = act_p.mark(act.activation(tmp1[:, :], tmp1[:, :], ACT.Exp, scale=-1.0))
                    wait(act, m)
                    m = act_p.mark(act.activation(tmp1[:, :], tmp1[:, :], ACT.Ln, bias=1.0))
                    wait(dve, m)
                    sp_mark = dve_p.mark(dve.scalar_tensor_tensor(
                        out=dt[:, k, :], in0=dt[:, k, :], scalar=0.0, in1=tmp1[:, :], op0=ALU.max, op1=ALU.add))
                    wait(dve, sp_mark, u_mark)
                    du_mark = dve_p.mark(dve.tensor_tensor(du[:, k, :], dt[:, k, :], u[:, k, :], ALU.mult))
                Y = [banks(4, 2), banks(6, 2)]

                def spread(ring, row):
                    ti, tile = ring.take()
                    for c in range(NC):
                        i, bank = spread_bank.take()
                        wait(pe, xdr_mark, xd_mark, pick_mark, spread_bank.free[i])
                        m = pe_p.mark(pe.matmul(bank, pickr[:, row, :], xdr[:, c * CH:(c + 1) * CH],
                                                start=True, stop=True))
                        wait(act, m, ring.free[ti])
                        r = act_p.mark(act.copy(tile[:, c * CH:(c + 1) * CH], bank))
                        spread_bank.free[i] = [r]
                    ring.free[ti] = []
                    return ti, tile, r

                def decays(k, n):
                    ai, decay = dA.take()
                    wait(act, sp_mark, A_mark, dA.free[ai])
                    return ai, decay, act_p.mark(act.activation(decay[:, :], dt[:, k, :], ACT.Exp,
                                                                scale=alog[:, k, n:n + 1]))

                def add_state(k, n, oi, hcn, o_mark):
                    wait(pe, o_mark, phase_free)
                    for c in range(NC):
                        ins = pe.matmul(Y[k][:, c * CH:(c + 1) * CH], ident[:, :], hcn[:, c * CH:(c + 1) * CH],
                                        start=(n == 0), stop=(n == NS - 1))
                    m = pe_p.mark(ins)
                    hc.free[oi] = [m]
                    return m

                ready = spread(bb, 0), spread(cc, NS), [decays(k, 0) for k in range(KI)]
                waiting = []
                for n in range(NS):
                    (bi, ball, b_mark), (ci, call, c_mark), decay_of = ready
                    if n + 1 < NS:
                        ready = spread(bb, n + 1), spread(cc, NS + n + 1), [decays(k, n + 1) for k in range(KI)]
                    for k in range(KI):
                        ai, decay, a_mark = decay_of[k]
                        gi, gain = dBu.take()
                        wait(dve, b_mark, du_mark, dBu.free[gi])
                        g_mark = dve_p.mark(dve.tensor_tensor(gain[:, :], ball[:, :], du[:, k, :], ALU.mult))
                        bb.free[bi] = [g_mark]
                        si, state = hs.take()
                        wait(dve, g_mark, a_mark, hs.free[si])
                        s_mark = dve_p.mark(dve.tensor_tensor_scan(state[:, :], decay[:, :], gain[:, :], 0.0,
                                                                   ALU.mult, ALU.add))
                        dA.free[ai], dBu.free[gi] = [s_mark], [s_mark]
                        oi, hcn = hc.take()
                        wait(pool, s_mark, c_mark, hc.free[oi])
                        pool_alone()
                        o_mark = pool_p.mark(pool.tensor_tensor(hcn[:, :], state[:, :], call[:, :], ALU.mult))
                        hs.free[si] = [o_mark]
                        cc.free[ci].append(o_mark)
                        waiting.append((k, n, oi, hcn, o_mark))
                        if len(waiting) > 2:
                            y_mark = add_state(*waiting.pop(0))
                for w in waiting:
                    y_mark = add_state(*w)
                for k in range(KI):
                    wait(dve, y_mark, ld["dsk"], zg_mark)
                    m = dve_p.mark(dve.scalar_tensor_tensor(out=du[:, k, :], in0=u[:, k, :], scalar=dsk[:, k:k + 1],
                                                            in1=Y[k], op0=ALU.mult, op1=ALU.add))
                    wait(dve, m)
                    g_mark = dve_p.mark(dve.tensor_tensor(du[:, k, :], du[:, k, :], zg[:, k, :], ALU.mult))
                for c in range(NC):
                    i, bank = work.take()
                    cs = slice(c * CH, (c + 1) * CH)
                    wait(pe, g_mark, ld["outp"], work.free[i])
                    for k in range(KI):
                        ins = pe.matmul(bank, outp[:, k, :], du[:, k, cs], start=(k == 0), stop=(k == KI - 1))
                    m = pe_p.mark(ins)
                    wait(act, m)
                    m = act_p.mark(act.copy(h1T[:, cs], bank))
                    work.free[i] = [m]
                    xs = x[:, b * NT + 4 * c:b * NT + 4 * c + 4, :]
                    wait(dve, ld["fc2b"])
                    n = dve_p.mark(dve.tensor_tensor(xs, xs, fc2b[:, :].unsqueeze(1).broadcast_to([P, 4, D]), ALU.add))
                    i, bank = work.take()
                    wait(pe, m, ld["fc2"], work.free[i])
                    for t in range(4):
                        tt = 4 * c + t
                        ins = pe.matmul(bank[:, t * P:(t + 1) * P], h1T[:, tt * P:(tt + 1) * P], fc2[:, :],
                                        start=True, stop=True)
                    m = pe_p.mark(ins)
                    wait(dve, m, n)
                    x_mark[b] = dve_p.mark(dve.tensor_tensor(xs, tile_bank(bank), xs, ALU.add))
                    work.free[i] = [x_mark[b]]
                phase_free = [m, x_mark[b]]

            for b in range(B):
                selective_scan(b)
        barrier()

        with ExitStack() as scope:
            def sba(name, shape, dt=F32):
                return sb(name, shape, dt, scope)

            w1, w2 = sba("e1_w1", [P, E1, F1]), sba("e1_w2", [P, M1, D])
            b1, b2 = sba("e1_b1", [P, M1]), sba("e1_b2", [P, D])
            all1 = sba("e1_ones", [P, P])
            gw, gb, rms = sba("e1_gw", [P, E1]), sba("e1_gb", [P, E1]), sba("e1_rms", [P, E1])
            lg, sq = sba("e1_lg", [P, NT, E1]), sba("e1_sq", [P, NT, E1])
            s1, s2 = sba("e1_s1", [P, NT]), sba("e1_s2", [P, NT])
            hT = Ring([sba(f"e1_h{i}", [P, M1, CH]) for i in range(2)])
            z = pool_set(b2[:, :], 0.0)
            z1 = pool_set(all1[:, :], 1.0)
            ld_g = [load("e1_gw", gw[:, :], a["e1_gw"]), load("e1_gb", gb[:, :], a["e1_gb"].partition_broadcast(P)),
                    load("e1_rms", rms[:, :], a["e1_rms"].partition_broadcast(P))]
            ld_w1 = [load("e1_w1", w1[:, :, :], a["e1_w1"].rearrange("e d f -> d e f")),
                     load("e1_b1", b1[:, :], a["e1_b1"])]
            ld_w2 = [load("e1_w2", w2[:, :, :], a["e1_w2"].rearrange("e (m p) d -> p (e m) d", p=P))]
            wait(sp, z)
            ld_w2.append(load("e1_b2", b2[0:E1, :], a["e1_b2"]))
            gate_free = []

            def wide(v):
                return v[:, :].unsqueeze(2).broadcast_to([P, NT, E1])

            def row(v):
                return v[:, :].unsqueeze(1).broadcast_to([P, NT, E1])

            def experts1(b):
                nonlocal gate_free
                layer_norm(b)
                i, bank = work.take()
                wait(pe, xnT_mark[b], ld_g, work.free[i])
                for t in range(NT):
                    ins = pe.matmul(bank[:, t * E1:(t + 1) * E1], xnT[:, b, t * P:(t + 1) * P], gw[:, :],
                                    start=True, stop=True)
                m = pe_p.mark(ins)
                wait(dve, m, ld_g, gate_free)
                m = dve_p.mark(dve.tensor_tensor(lg[:, :, :], bank[:, 0:NT * E1].rearrange("p (t e) -> p t e", e=E1),
                                                 row(gb), ALU.add))
                work.free[i] = [m]
                wait(dve, m)
                m = dve_p.mark(dve.tensor_tensor(sq[:, :, :], lg[:, :, :], lg[:, :, :], ALU.mult))
                wait(dve, m)
                m = dve_p.mark(dve.tensor_reduce(s1[:, :], sq[:, :, :], AXX, ALU.add))
                wait(dve, m)
                m = dve_p.mark(dve.tensor_scalar(s1[:, :], s1[:, :], 1.0 / E1, F32_EPS, ALU.mult, ALU.add))
                wait(act, m)
                m = act_p.mark(act.activation(s1[:, :], s1[:, :], ACT.Sqrt))
                wait(dve, m)
                m = dve_p.mark(dve.reciprocal(s1[:, :], s1[:, :]))
                wait(dve, m)
                m = dve_p.mark(dve.tensor_tensor(lg[:, :, :], lg[:, :, :], wide(s1), ALU.mult))
                wait(dve, m)
                m = dve_p.mark(dve.tensor_tensor(lg[:, :, :], lg[:, :, :], row(rms), ALU.mult))
                wait(dve, m)
                m = dve_p.mark(dve.tensor_reduce(s2[:, :], lg[:, :, :], AXX, ALU.max))
                wait(dve, m)
                m = dve_p.mark(dve.tensor_tensor(lg[:, :, :], lg[:, :, :], wide(s2), ALU.subtract))
                wait(act, m)
                m = act_p.mark(act.activation(lg[:, :, :], lg[:, :, :], ACT.Exp, scale=2.0))
                wait(dve, m)
                m = dve_p.mark(dve.tensor_reduce(s1[:, :], lg[:, :, :], AXX, ALU.add))
                wait(dve, m)
                m = dve_p.mark(dve.reciprocal(s1[:, :], s1[:, :]))
                wait(dve, m)
                m = dve_p.mark(dve.tensor_scalar(s2[:, :], s1[:, :], GATE_EPS, None, ALU.add))
                wait(dve, m)
                m = dve_p.mark(dve.reciprocal(s2[:, :], s2[:, :]))
                wait(dve, m)
                norm_mark = dve_p.mark(dve.tensor_tensor(s2[:, :], s2[:, :], s1[:, :], ALU.mult))

                def hidden(c):
                    k, h = hT.take()
                    for m_ in range(M1):
                        i, bank = hid.take()
                        e, f = divmod(m_, F1 // P)
                        wait(pe, ld_w1, hid.free[i])
                        m = pe_p.mark(pe.matmul(bank, w1[:, e, f * P:(f + 1) * P], xnT[:, b, c * CH:(c + 1) * CH],
                                                start=True, stop=True))
                        wait(act, m, ld_w1, hT.free[k])
                        g = act_p.mark(act.activation(h[:, m_, :], bank, ACT.Gelu, bias=b1[:, m_:m_ + 1]))
                        hid.free[i] = [g]
                    return k, h, g

                def down(c, k, h, g):
                    i, bank = ybank.take()
                    wait(pe, g, ld_w2, z1, ybank.free[i])
                    for t in range(4):
                        for m_ in range(M1):
                            pe.matmul(bank[:, t * P:(t + 1) * P], h[:, m_, t * P:(t + 1) * P], w2[:, m_, :],
                                      start=(m_ == 0), stop=False)
                        ins = pe.matmul(bank[:, t * P:(t + 1) * P], all1[:, :], b2[:, :], start=False, stop=True)
                    m = pe_p.mark(ins)
                    hT.free[k] = [m]
                    for t in range(4):
                        tt = 4 * c + t
                        xs = x[:, b * NT + tt, :]
                        wait(dve, m, norm_mark)
                        r = dve_p.mark(dve.scalar_tensor_tensor(
                            out=xs, in0=bank[:, t * P:(t + 1) * P], scalar=s2[:, tt:tt + 1],
                            in1=xs, op0=ALU.mult, op1=ALU.add))
                    ybank.free[i] = [r]
                    wait(sp, r)
                    stores.append(progress(f"st{b}{c}", 16).mark(sp.dma_start(
                        out_d[:, b * NT + 4 * c:b * NT + 4 * c + 4, :], x[:, b * NT + 4 * c:b * NT + 4 * c + 4, :])))
                    return r

                held = [(c, *hidden(c)) for c in range(NC)]
                for h in held:
                    r = down(*h)
                gate_free = [r]

            stores = []
            for b in range(B):
                experts1(b)
            wait(sp, stores)



def _layout(i):
    f = {k: np.asarray(v) for k, v in i.items()}
    A, G, S, M = "L0_attn_", "L0_ffn_", "L1_attn_", "L1_ffn_"
    heads = lambda w: w.transpose(2, 0, 1).reshape(D, H * DH)
    cols = lambda v, k: v.reshape(k, P).T
    o = {
        "x": f[A + "x"].reshape(B * SEQ, D),
        "ident": np.eye(P, dtype=np.float32),
        "wq": heads(f[A + "W_Q"]), "wk": heads(f[A + "W_K"]), "wv": heads(f[A + "W_V"]),
        "bq": cols(f[A + "b_Q"], NPAIR), "bk": cols(f[A + "b_K"], NPAIR),
        "bv": f[A + "b_V"].reshape(H * DH),
        "wo": f[A + "W_O"].transpose(0, 2, 1).reshape(NPAIR, P, D).transpose(1, 0, 2).reshape(P, NPAIR * D),
        "bo": f[A + "b_O"],
        "rank": np.arange(E0, 0, -1, dtype=np.float32),
        "e0_wg": f[G + "wg"], "e0_w1": f[G + "w1"], "e0_w2": f[G + "w2"], "e0_b2": f[G + "b2"],
        "e0_b1": cols(f[G + "b1"], E0 * M0),
        "fc1": f[S + "fc1_w"].T, "fc1b": f[S + "fc1_b"].reshape(P, 1), "inp": f[S + "in_proj_w"].T,
        "cw": f[S + "conv_w"].reshape(KI, P, DCONV).transpose(1, 0, 2), "cb": cols(f[S + "conv_b"], KI),
        "dtb": cols(f[S + "dt_proj_b"], KI),
        "alog": f[S + "A_log"].reshape(KI, P, NS).transpose(1, 0, 2), "dsk": cols(f[S + "D"], KI),
        "outp": f[S + "out_proj_w"].T.reshape(KI, P, D).transpose(1, 0, 2),
        "fc2": f[S + "fc2_w"].T, "fc2b": f[S + "fc2_b"],
        "e1_gw": f[M + "gate_w"].T, "e1_gb": f[M + "gate_b"], "e1_rms": f[M + "rms_w"],
        "e1_w1": f[M + "w1"], "e1_b1": cols(f[M + "b1"], M1), "e1_w2": f[M + "w2"], "e1_b2": f[M + "b2"],
    }
    sel = np.zeros((P, NT, P), np.float32)
    for t in range(NT):
        sel[t, t, :LO] = 1.0
        sel[NT + t, t, LO:] = 1.0
    o["sel"] = sel
    wred = np.zeros((P, P), np.float32)
    wred[:, :GATE] = f[G + "wg_red"].T
    o["e0_wred"] = wred
    rows = DTR + 2 * NS
    xpj = np.zeros((P, KI, P), np.float32)
    xw = f[S + "x_proj_w"].T.reshape(KI, P, rows).transpose(1, 0, 2)
    xpj[:, :, :rows] = xw
    xpj[:, :, 64:64 + rows] = xw
    o["xpj"] = xpj
    dtp = np.zeros((P, DI), np.float32)
    dtp[:DTR] = f[S + "dt_proj_w"].T
    o["dtp"] = dtp
    pick = np.zeros((P, 2 * NS, P), np.float32)
    for n in range(2 * NS):
        pick[DTR + n, n, :] = 1.0
        pick[64 + DTR + n, n, :] = 1.0
    o["pick"] = pick
    return {k: np.ascontiguousarray(v) for k, v in o.items()}


def kernel(**inputs):
    from concourse import bacc
    from concourse.bass_utils import run_bass_kernel_spmd

    arrays = _layout(inputs)
    nc = bacc.Bacc("TRN2", target_bir_lowering=False, num_devices=1)
    ins = {k: nc.dram_tensor("in_" + k, v.shape, mybir.dt.from_np(v.dtype), kind="ExternalInput").ap()
           for k, v in arrays.items()}
    out = nc.dram_tensor("out_x", (B * SEQ, D), F32, kind="ExternalOutput").ap()
    two_layer_program(nc, ins, out)
    r = run_bass_kernel_spmd(nc, [{"in_" + k: v for k, v in arrays.items()}], core_ids=[0])
    return r.results[0]["out_x"].reshape(B, SEQ, D)
```

```python
from contextlib import ExitStack
from itertools import chain

import numpy as np

import concourse.bass as bass
from concourse import mybir

F32 = mybir.dt.float32
F32R = mybir.dt.float32r
ACT = mybir.ActivationFunctionType
ALU = mybir.AluOpType
AXX = mybir.AxisListType.X

P = 128
B, SEQ, D = 2, 1024, 128
NT = SEQ // P
CH = 512
NC = SEQ // CH
H, DH = 16, 64
NPAIR = H // 2
E0, F0, GATE = 8, 512, 16
M0 = F0 // P
DI, NS, DTR, DCONV = 256, 16, 8, 4
KI = DI // P
E1, F1 = 8, 256
M1 = E1 * F1 // P
LO = 64
LN_EPS, NORM_EPS, GATE_EPS = 1e-5, 1e-4, 1e-6
F32_EPS = float(np.finfo(np.float32).eps)


class Progress:

    def __init__(self, sem, step=1):
        self.sem, self.step, self.count = sem, step, 0

    def mark(self, instruction):
        instruction.then_inc(self.sem, self.step)
        self.count += self.step
        return (self, self.count)


class Waits:

    def __init__(self):
        self.seen = {}

    def __call__(self, engine, *marks):
        for m in marks:
            if m is None:
                continue
            if isinstance(m, list):
                self(engine, *m)
                continue
            progress, level = m
            key = (id(engine), progress)
            if self.seen.get(key, 0) < level:
                engine.wait_ge(progress.sem, level)
                self.seen[key] = level


class Buffer:

    def __init__(self, ap):
        self.ap, self.free = ap, []


class Ring:

    def __init__(self, buffers):
        self.slots = [b if isinstance(b, Buffer) else Buffer(b) for b in buffers]
        self.at = -1

    def take(self):
        self.at = (self.at + 1) % len(self.slots)
        return self.slots[self.at], self.slots[self.at].ap


def interleave(main, side, ratio):
    due = 0.0
    for _ in main:
        due += ratio
        while due >= 1.0:
            due -= 1.0
            if next(side, "end") == "end":
                due = float("-inf")
    for _ in side:
        pass


def two_layer_program(nc, a, out):
    pe, act, dve, pool, sp = nc.tensor, nc.scalar, nc.vector, nc.gpsimd, nc.sync
    wait = Waits()
    with ExitStack() as ctx:
        def sb(name, shape, dt=F32, scope=ctx):
            return scope.enter_context(nc.sbuf_tensor(name, shape, dt))

        def progress(name, step=1):
            return Progress(ctx.enter_context(nc.semaphore(name)), step)

        pe_p, act_p, dve_p, pool_p = (progress(n) for n in ("pe_done", "act_done", "dve_done", "pool_done"))

        def pool_alone():
            wait(pool, (pool_p, pool_p.count))

        def pool_set(dst, value):
            pool_alone()
            return pool_p.mark(pool.memset(dst, value))

        psum = ctx.enter_context(nc.psum_tensor("psum", [P, 8 * CH], F32))

        def banks(first, n=1):
            return psum[:, first * CH:(first + n) * CH]

        bank_of = [Buffer(banks(i)) for i in range(8)]
        work = Ring(bank_of[0:2])

        def load(name, dst, src):
            return progress("ld_" + name, 16).mark(sp.dma_start(dst, src))

        x = sb("x", [P, B * NT, D])
        xnT = sb("xnT", [P, B, SEQ])
        ident = sb("ident", [P, P])
        xrows = sb("xrows", [P, B * NT, D])
        stats = sb("stats", [P, NT, 6])
        mv = sb("mv", [P, NT, 2])
        rstd = sb("rstd", [P, NT])
        std = sb("std", [P, NT])
        x_d = a["x"].rearrange("(t p) d -> p t d", p=P)
        out_d = out.rearrange("(t p) d -> p t d", p=P)
        ld_x = [load(f"x{b}", x[:, b * NT:(b + 1) * NT, :], x_d[:, b * NT:(b + 1) * NT, :]) for b in range(B)]
        ld_ident = load("ident", ident[:, :], a["ident"])
        x_mark = list(ld_x)
        xnT_mark = [[], []]
        xnT_free = [[], []]
        ln_free = []

        def layer_norm_steps(b):
            nonlocal ln_free
            xn = xrows[:, b * NT:(b + 1) * NT, :]
            wait(dve, x_mark[b], *ln_free)
            for t in range(NT):
                m = dve_p.mark(dve.bn_stats(stats[:, t, :], x[:, b * NT + t, :]))
            wait(dve, m)
            for t in range(NT):
                m = dve_p.mark(dve.bn_aggr(mv[:, t, :], stats[:, t, :]))
            wait(dve, m)
            m = dve_p.mark(dve.tensor_scalar(std[:, :], mv[:, :, 1], LN_EPS, None, ALU.add))
            wait(act, m)
            m = act_p.mark(act.activation(std[:, :], std[:, :], ACT.Sqrt))
            yield
            wait(dve, m)
            m = dve_p.mark(dve.reciprocal(rstd[:, :], std[:, :]))
            wait(dve, m)
            rows = []
            for t in range(NT):
                rows.append(dve_p.mark(dve.tensor_scalar(
                    xn[:, t, :], x[:, b * NT + t, :], mv[:, t, 0:1], rstd[:, t:t + 1], ALU.subtract, ALU.mult)))
            yield
            ends = []
            for g in range(NT // 4):
                slot, bank = work.take()
                wait(pe, rows[4 * g + 3], ld_ident, slot.free)
                for t in range(4):
                    ins = pe.transpose(bank[:, t * P:(t + 1) * P], xn[:, 4 * g + t, :], ident[:, :])
                m = pe_p.mark(ins)
                wait(act, m, *xnT_free[b])
                ends.append(act_p.mark(act.copy(xnT[:, b, g * CH:(g + 1) * CH], bank)))
                slot.free = [ends[-1]]
            ln_free = [m]
            xnT_mark[b] = [ends[-1]]
            xnT_free[b] = []

        def layer_norm(b):
            for _ in layer_norm_steps(b):
                pass

        wred = sb("e0_wred", [P, P])
        wg, wgsq = sb("e0_wg", [P, P]), sb("e0_wgsq", [E0, GATE])
        wgn = sb("e0_wgn", [E0, 1])
        wgu = sb("e0_wgu", [P, E0])
        logits = sb("e0_logits", [P, B * NT, E0])
        logits_mark = [None] * B
        ld_wred = load("e0_wred", wred[:, :], a["e0_wred"])
        z_wg = pool_set(wg[:, :], 0.0)
        wait(sp, z_wg)
        ld_wg = load("e0_wg", wg[0:E0, 0:GATE], a["e0_wg"])

        wgu_mark = None

        def gate_directions():
            nonlocal wgu_mark
            wait(dve, ld_wg)
            m = dve_p.mark(dve.tensor_tensor(wgsq[:, :], wg[0:E0, 0:GATE], wg[0:E0, 0:GATE], ALU.mult))
            wait(dve, m)
            m = dve_p.mark(dve.tensor_reduce(wgn[:, :], wgsq[:, :], AXX, ALU.add))
            wait(act, m)
            m = act_p.mark(act.activation(wgn[:, :], wgn[:, :], ACT.Sqrt))
            wait(dve, m)
            m = dve_p.mark(dve.tensor_scalar(wgn[:, :], wgn[:, :], NORM_EPS, None, ALU.max))
            wait(dve, m)
            m = dve_p.mark(dve.reciprocal(wgn[:, :], wgn[:, :]))
            wait(dve, m)
            m = dve_p.mark(dve.tensor_scalar(wg[0:E0, 0:GATE], wg[0:E0, 0:GATE], wgn[:, 0:1], None, ALU.mult))
            slot, bank = work.take()
            wait(pe, m, z_wg, slot.free)
            m = pe_p.mark(pe.transpose(bank[:, 0:P], wg[:, :], ident[:, :]))
            wait(dve, m)
            wgu_mark = dve_p.mark(dve.tensor_copy(wgu[:, :], bank[:, 0:E0]))
            slot.free = [wgu_mark]

        def gate_logits(b):
            yield from layer_norm_steps(b)
            yield
            for c in range(NC):
                slot, bank = work.take()
                cs = slice(c * CH, (c + 1) * CH)
                wait(pe, xnT_mark[b], ld_wred, slot.free)
                m = pe_p.mark(pe.matmul(bank, wred[:, :], xnT[:, b, cs], start=True, stop=True))
                wait(act, m)
                xr_mark = act_p.mark(act.copy(xnT[:, b, cs], bank))
                slot.free = [xr_mark]
                yield
            slot, bank = work.take()
            wait(pe, xr_mark, wgu_mark, slot.free)
            for t in range(NT):
                ins = pe.matmul(bank[:, t * E0:(t + 1) * E0], xnT[:, b, t * P:(t + 1) * P], wgu[:, :],
                                start=True, stop=True)
            m = pe_p.mark(ins)
            xnT_free[b] = [m]
            wait(dve, m)
            logits_mark[b] = dve_p.mark(dve.tensor_copy(
                logits[:, b * NT:(b + 1) * NT, :], bank[:, 0:NT * E0].rearrange("p (t e) -> p t e", e=E0)))
            slot.free = [logits_mark[b]]

        with ExitStack() as scope:
            def sba(name, shape, dt=F32):
                return sb(name, shape, dt, scope)

            wq, wk, wv, wo = (sba(n, [P, H * DH]) for n in ("wq", "wk", "wv", "wo"))
            bq, bk = sba("bq", [P, NPAIR]), sba("bk", [P, NPAIR])
            bv, bo = sba("bv", [P, H * DH]), sba("bo", [P, D])
            ones = sba("ones", [P, LO])
            V = sba("V", [P, NT, H * DH])
            K1, K2, Q1, Q2 = ([[sba(f"{n}{q}{s}", [P, SEQ], F32R) for s in range(2)] for q in range(2)]
                              for n in ("K1_", "K2_", "Q1_", "Q2_"))
            NPB = 3
            prob = [Ring([sba(f"prob{s}{i}", [P, SEQ]) for i in range(NPB)]) for s in range(2)]
            psums = [[sba(f"psums{q}{s}", [P, SEQ]) for s in range(2)] for q in range(2)]
            mx = sba("mx", [P, 2, NT, NC])
            nmx = [sba(f"nmx{s}", [P, P]) for s in range(2)]
            mrow = [sba(f"mrow{s}", [P, P], F32R) for s in range(2)]
            inv = sba("inv", [P, 2, SEQ // P])
            oraw = sba("oraw", [P, SEQ])
            onorm = sba("onorm", [P, SEQ])
            inv_d = nc.dram_tensor("inverse_sums", (2, SEQ), F32, kind="Internal").ap()

            ld_wk = load("wk", wk[:, :], a["wk"])
            ld_wq = load("wq", wq[:, :], a["wq"])
            ld_b = [load("bk", bk[:, :], a["bk"]), load("bq", bq[:, :], a["bq"])]
            ld_wv = [load("wv", wv[:, :], a["wv"]), load("bv", bv[:, :], a["bv"].partition_broadcast(P))]
            ld_wo = [load("wo", wo[:, :], a["wo"]), load("bo", bo[:, :], a["bo"].partition_broadcast(P))]

            HALF = [slice(0, LO), slice(LO, P)]
            REST = [slice(LO, P), slice(0, LO)]
            GROW = [slice(LO, LO + 1), slice(0, 1)]
            for q in range(2):
                for s in range(2):
                    pool_set(Q2[q][s][REST[s], :].bitcast(F32), 0.0)
                    pool_set(K2[q][s][REST[s], :].bitcast(F32), 0.0)
            pool_set(ones[:, :], 1.0)
            for z in (nmx[0], nmx[1]):
                pool_set(z[:, :], 0.0)
            for q in range(2):
                for s in range(2):
                    init = pool_set(K2[q][s][GROW[s], :].bitcast(F32), 1.0)

            guard = [[progress(f"guard{q}{s}", 16) for s in range(2)] for q in range(2)]
            guard_mark = [[None, None], [None, None]]
            qk_mark = [[{}, {}], [{}, {}]]
            score_mark = [[], []]
            S = [banks(2, 2), banks(4, 2)]
            S_free = [[], []]
            O = banks(6, 2)
            O_free = []
            oraw_free, onorm_free = [], []
            sum_cols, inv_out, inv_rows = (progress(n, 16) for n in ("sum_cols", "inv_out", "inv_rows"))
            sums_mark = inv_mark = None
            mx_free, nmx_free, mrow_free = [[], []], [[], []], [[], []]
            psums_mark, psums_free = [[None, None], [None, None]], [[], []]
            prob_mark = {}
            pv_end = {}
            V_mark = [None] * NT
            pv_mark = [None] * NT

            def values(b, t):
                for c in range(2):
                    slot, bank = work.take()
                    wait(pe, xnT_mark[b], ld_wv, slot.free)
                    m = pe_p.mark(pe.matmul(bank, xnT[:, b, t * P:(t + 1) * P], wv[:, c * CH:(c + 1) * CH],
                                            start=True, stop=True))
                    wait(dve, m, ld_wv, pv_mark[t])
                    V_mark[t] = dve_p.mark(dve.tensor_tensor(V[:, t, c * CH:(c + 1) * CH], bank,
                                                             bv[:, c * CH:(c + 1) * CH], ALU.add))
                    slot.free = [V_mark[t]]

            def project(pair, kind, c):
                b, p = divmod(pair, NPAIR)
                q = pair % 2
                w, bias, full, part = (wk, bk, K1, K2) if kind == "k" else (wq, bq, Q1, Q2)
                cs = slice(c * CH, (c + 1) * CH)
                slot, bank = work.take()
                wait(pe, xnT_mark[b], ld_wk, ld_wq, slot.free)
                m = pe_p.mark(pe.matmul(bank, w[:, 2 * p * DH:(2 * p + 2) * DH], xnT[:, b, cs], start=True, stop=True))
                wait(act, m, ld_b, score_mark[q])
                hi = [act_p.mark(act.activation(full[q][s][HALF[s], cs], bank[HALF[s], :], ACT.Identity,
                                                bias=bias[HALF[s], p:p + 1])) for s in range(2)]
                wait(dve, m, ld_b, score_mark[q], init)
                for s in range(2):
                    wait(dve, hi)
                    lo = full[q][s][REST[s], cs] if kind == "k" else part[q][s][HALF[s], cs]
                    m = dve_p.mark(dve.scalar_tensor_tensor(
                        out=lo, in0=bank[HALF[s], :], scalar=bias[HALF[s], p:p + 1],
                        in1=full[q][s][HALF[s], cs], op0=ALU.add, op1=ALU.subtract))
                    copy = part[q][s][HALF[s], cs] if kind == "k" else full[q][s][REST[s], cs]
                    n = dve_p.mark(dve.tensor_copy(copy, full[q][s][HALF[s], cs]))
                    qk_mark[q][s][kind, c] = [n]
                slot.free = [m]

            def row_max(pair, s, t, c):
                q = pair % 2
                slot, bank = work.take()
                wait(pe, qk_mark[q][s]["k", c], qk_mark[q][s]["q", t * P // CH], slot.free)
                m = pe_p.mark(pe.matmul(bank, Q1[q][s][:, t * P:(t + 1) * P], K1[q][s][:, c * CH:(c + 1) * CH],
                                        start=True, stop=True))
                wait(dve, m, mx_free[s])
                r = dve_p.mark(dve.tensor_reduce(mx[:, s, t, c:c + 1], bank, AXX, ALU.max))
                slot.free = [r]
                max_mark[s] = r

            def guard_columns(s):
                wait(dve, max_mark[s], nmx_free[s], init)
                nmx_mark[s] = dve_p.mark(dve.tensor_reduce(nmx[s][:, 0:NT], mx[:, s, :, :], AXX, ALU.max, negate=True))
                mx_free[s] = [nmx_mark[s]]

            def guard_row(pair, s):
                q = pair % 2
                slot, bank = work.take()
                wait(pe, nmx_mark[s], ld_ident, slot.free)
                m = pe_p.mark(pe.transpose(bank[:, 0:P], nmx[s][:, :], ident[:, :]))
                nmx_free[s] = [m]
                wait(dve, m, mrow_free[s])
                m = dve_p.mark(dve.tensor_copy(mrow[s][0:NT, :], bank[0:NT, 0:P]))
                slot.free = [m]
                wait(sp, m, score_mark[q], init)
                guard_mark[q][s] = guard[q][s].mark(sp.dma_start(
                    Q2[q][s][GROW[s], :].rearrange("o (t k) -> o t k", t=NT).bitcast(F32),
                    mrow[s][0:NT, :].bitcast(F32)))
                mrow_free[s] = [guard_mark[q][s]]

            def scores_hi(pair, j, s):
                q = pair % 2
                wait(pe, list(qk_mark[q][s].values()), S_free[s])
                for c in range(NC):
                    pe.matmul(S[s][:, c * CH:(c + 1) * CH], K1[q][s][:, j * P:(j + 1) * P],
                              Q1[q][s][:, c * CH:(c + 1) * CH], start=True, stop=False)

            def scores_lo(pair, j, s):
                q = pair % 2
                wait(pe, guard_mark[q][s], init)
                for c in range(NC):
                    ins = pe.matmul(S[s][:, c * CH:(c + 1) * CH], K2[q][s][:, j * P:(j + 1) * P],
                                    Q2[q][s][:, c * CH:(c + 1) * CH], start=False, stop=True)
                m = pe_p.mark(ins)
                score_mark[q] = [m]
                slot, weights = prob[s].take()
                wait(act, m, slot.free)
                e = act_p.mark(act.activation(weights[:, :], S[s], ACT.Exp, scale=float(DH) ** -0.5))
                S_free[s] = [e]
                prob_mark[pair, j, s] = (slot, e)
                if pair == npairs - 1 and s == 1:
                    if j:
                        sum_up(pair, j - 1, s)
                else:
                    sum_up(pair, j, s)

            def sum_up(pair, j, s):
                q = pair % 2
                slot, e = prob_mark[pair, j, s]
                weights = slot.ap
                if j == 0:
                    return
                total = psums[q][s]
                before = prob_mark[pair, 0, s][0].ap if j == 1 else total
                engine, done = (dve, dve_p) if s == 1 and pair == npairs - 1 else (pool, pool_p)
                wait(engine, e, prob_mark[pair, 0, s][1], psums_free[q], psums_mark[q][s])
                if engine is pool:
                    pool_alone()
                psums_mark[q][s] = done.mark(engine.tensor_tensor(total[:, :], before[:, :], weights[:, :], ALU.add))
                if j == 1:
                    prob_mark[pair, 0, s][0].free.append(psums_mark[q][s])
                slot.free = [psums_mark[q][s]]

            def weighted_values(pair, j, c):
                p = pair % NPAIR
                slots = [prob_mark[pair, j, s] for s in range(2)]
                wait(pe, V_mark[j], *(e for _, e in slots))
                if j == 0:
                    wait(pe, O_free)
                for s in range(2):
                    h = 2 * p + s
                    ins = pe.matmul(O[s * LO:(s + 1) * LO, c * CH:(c + 1) * CH], V[:, j, h * DH:(h + 1) * DH],
                                    slots[s][0].ap[:, c * CH:(c + 1) * CH],
                                    start=(j == 0), stop=(j == NT - 1))
                if c == NC - 1:
                    m = pv_mark[j] = pe_p.mark(ins)
                    for s in range(2):
                        slots[s][0].free = slots[s][0].free + [m]
                    if j == NT - 1:
                        pv_end[pair] = m

            def take_out(pair):
                nonlocal O_free
                wait(act, pv_end[pair], oraw_free)
                O_free = [act_p.mark(act.copy(oraw[:, :], O))]

            max_mark, nmx_mark = [None, None], [None, None]
            onorm_mark = None

            def sum_weights(pair, c):
                nonlocal sums_mark
                q = pair % 2
                slot, bank = work.take()
                wait(pe, psums_mark[q], slot.free, init)
                for s in range(2):
                    ins = pe.matmul(bank[s * LO:(s + 1) * LO, :], ones[:, :], psums[q][s][:, c * CH:(c + 1) * CH],
                                    start=True, stop=True)
                m = pe_p.mark(ins)
                psums_free[q] = [m]
                wait(act, m, onorm_free)
                sums_mark = act_p.mark(act.copy(onorm[:, c * CH:(c + 1) * CH], bank))
                slot.free = [sums_mark]

            def sums_to_columns():
                wait(sp, sums_mark, inv_mark)
                for s in range(2):
                    m = sum_cols.mark(sp.dma_start(inv[:, s, :], onorm[s * LO:s * LO + 1, :]
                                                   .rearrange("o (p i) -> o p i", p=P)))

            def invert_sums():
                nonlocal inv_mark
                wait(dve, (sum_cols, sum_cols.count))
                m = dve_p.mark(dve.reciprocal(inv[:, :, :], inv[:, :, :]))
                wait(sp, m, inv_mark)
                m = inv_out.mark(sp.dma_start(inv_d.rearrange("s (p i) -> p s i", p=P), inv[:, :, :]))
                wait(sp, m)
                for s in range(2):
                    inv_mark = inv_rows.mark(sp.dma_start(onorm[s * LO:(s + 1) * LO, :],
                                                          inv_d[s, :].partition_broadcast(LO)))

            def normalise(pair, c):
                nonlocal oraw_free, onorm_mark
                wait(dve, inv_mark, O_free)
                cs = slice(c * CH, (c + 1) * CH)
                onorm_mark = dve_p.mark(dve.tensor_tensor(onorm[:, cs], onorm[:, cs], oraw[:, cs], ALU.mult))
                oraw_free = [onorm_mark]

            def project_out(pair, c):
                nonlocal onorm_free
                b, p = divmod(pair, NPAIR)
                slot, bank = work.take()
                wait(pe, onorm_mark, ld_wo, slot.free)
                for t in range(4):
                    ins = pe.matmul(bank[:, t * P:(t + 1) * P], onorm[:, (4 * c + t) * P:(4 * c + t + 1) * P],
                                    wo[:, p * D:(p + 1) * D], start=True, stop=True)
                m = pe_p.mark(ins)
                wait(dve, m, x_mark[b])
                xs = x[:, b * NT + 4 * c:b * NT + 4 * c + 4, :]
                x_mark[b] = dve_p.mark(dve.tensor_tensor(xs, bank.rearrange("p (t d) -> p t d", d=D), xs, ALU.add))
                slot.free = [x_mark[b]]
                onorm_free = [m]

            def start_batch(b):
                layer_norm(b)
                wait(dve, ld_wo, (dve_p, dve_p.count))
                xs = x[:, b * NT:(b + 1) * NT, :]
                x_mark[b] = dve_p.mark(dve.tensor_tensor(
                    xs, xs, bo[:, :].unsqueeze(1).broadcast_to([P, NT, D]), ALU.add))

            END_AT, GUARD_BACK = (4, 8, 12, 18, 27, 29, 33, 37), 14

            def side_work(pair, nxt):
                early, late = [], []
                if nxt is None and pair == npairs - 2:
                    late = [lambda: None] * (2 * NT * NC + 4)
                if nxt is not None:
                    early = [lambda k=k, c=c: project(nxt, k, c) for k in "kq" for c in range(NC)]
                    for s in range(2):
                        late += [lambda s=s, t=t, c=c: row_max(nxt, s, t, c)
                                 for ts in (range(NT // 2), range(NT // 2, NT)) for c in range(NC) for t in ts]
                        late.append(lambda s=s: guard_columns(s))
                    late.insert(len(late) - GUARD_BACK, lambda: guard_row(nxt, 0))
                if pair is not None:
                    ends = [lambda c=c: sum_weights(pair, c) for c in range(NC)] + [sums_to_columns, invert_sums]
                    ends += [lambda f=f, c=c: f(pair, c) for f in (normalise, project_out) for c in range(NC)]
                    for at, f in zip(END_AT, ends):
                        late.insert(at, f)
                if nxt is not None:
                    late.append(lambda: guard_row(nxt, 1))
                elif pair == npairs - 2:
                    steps = gate_logits(0)
                    early.append(gate_directions)
                    for at in range(len(late) - 2, 2, -4):
                        late.insert(at, lambda: next(steps, None))
                return early, late

            npairs = B * NPAIR
            start_batch(0)
            first = side_work(None, 0)
            for n, job in enumerate(first[0] + first[1]):
                job()
                if n % 4 == 3 and n // 4 < NT:
                    values(0, n // 4)
            for pair in range(npairs):
                early, late = side_work(pair - 1 if pair else None, pair + 1 if pair + 1 < npairs else None)
                GAP = 3
                slots = 6 * NT
                at, nearly, nlate = 0, GAP * len(early) + 1, len(late)

                def side():
                    nonlocal at
                    if at < nearly:
                        if at % GAP == 0 and early:
                            early.pop(0)()
                    else:
                        due = nlate * (at - nearly + 1) / (slots - nearly)
                        while late and nlate - len(late) < due:
                            late.pop(0)()
                    at += 1

                for j in range(NT):
                    before = (pair, j - 1) if j else (pair - 1, NT - 1)
                    for s in range(2):
                        scores_hi(pair, j, s)
                        side()
                        scores_lo(pair, j, s)
                        side()
                        if before[0] >= 0:
                            weighted_values(*before, s)
                            if s == 1 and j == 0:
                                take_out(pair - 1)
                        side()
                    if before[0] == NPAIR - 1:
                        values(1, before[1])
                    if pair == 2 and j == 4:
                        start_batch(1)
            sum_up(npairs - 1, NT - 1, 1)
            for c in range(NC):
                weighted_values(npairs - 1, NT - 1, c)
            take_out(npairs - 1)
            for job in side_work(npairs - 1, None)[1]:
                job()

        def barrier(*marks):
            ends = [(p, p.count) for p in (pe_p, act_p, dve_p, pool_p)] + list(marks)
            for engine in (pe, act, dve, pool, sp):
                wait(engine, ends)

        barrier()
        def tile_bank(bank):
            return bank.rearrange("p (t d) -> p t d", d=D)

        ew1, ew2 = sb("e1_w1", [P, E1, F1]), sb("e1_w2", [P, M1, D])
        eb1, eb2 = sb("e1_b1", [P, M1]), sb("e1_b2", [P, E1])
        gw, gb, rms = sb("e1_gw", [P, E1]), sb("e1_gb", [P, E1]), sb("e1_rms", [P, E1])
        fc1, inp = sb("fc1", [P, D]), sb("inp", [P, 2 * DI])
        fc1b = sb("fc1b", [P, 1])
        cw, cb = sb("cw", [P, KI, DCONV]), sb("cb", [P, KI])
        xpj = sb("xpj", [P, KI, P])
        dtp, dtb = sb("dtp", [P, DI]), sb("dtb", [P, KI])
        alog, dsk = sb("alog", [P, KI, NS]), sb("dsk", [P, KI])
        outp, fc2, fc2b = sb("outp", [P, KI, D]), sb("fc2", [P, D]), sb("fc2b", [P, D])
        pick = sb("pick", [P, 2 * NS])
        pickr = sb("pickr", [P, 2 * NS], F32R)
        ld = {}

        def load_late_weights():
            for name, t in (("fc1", fc1), ("fc1b", fc1b), ("inp", inp), ("cw", cw), ("cb", cb), ("xpj", xpj),
                            ("dtp", dtp), ("dtb", dtb), ("alog", alog), ("dsk", dsk), ("outp", outp), ("fc2", fc2),
                            ("pick", pick), ("e1_gw", gw), ("e1_b1", eb1), ("e1_b2", eb2)):
                ld[name] = load(name, t[:], a[name])
            for name, t in (("fc2b", fc2b), ("e1_gb", gb), ("e1_rms", rms)):
                ld[name] = load(name, t[:], a[name].partition_broadcast(P))
            ld["e1_w1"] = load("e1_w1", ew1[:, :, :], a["e1_w1"].rearrange("e d f -> d e f"))
            ld["e1_w2"] = load("e1_w2", ew2[:, :, :], a["e1_w2"].rearrange("e (m p) d -> p (e m) d", p=P))

        AT = B * NT
        I32, U32 = mybir.dt.int32, mybir.dt.uint32
        posi = sb("posi", [P, AT], I32)
        score = sb("score", [P, AT])
        yback = sb("yback", [P, AT, D])
        lg1, sq1 = sb("e1_lg", [P, NT, E1]), sb("e1_sq", [P, NT, E1])
        s1 = sb("e1_s1", [P, NT])
        gates = [sb(f"e1_gate{b}", [P, NT]) for b in range(B)]

        with ExitStack() as scope:
            def sba(name, shape, dt=F32):
                return sb(name, shape, dt, scope)

            TE = AT * E0
            NSLOT = AT + E0 - 1
            ROW = M0 * P + M0 + M0 * D + D
            O_B1, O_W2, O_B2 = M0 * P, M0 * P + M0, M0 * P + M0 + M0 * D
            slots_in = nc.dram_tensor("slots_in", (NSLOT * P, D), F32, kind="Internal").ap()
            slots_out = nc.dram_tensor("slots_out", (NSLOT * P, D), F32, kind="Internal").ap()

            rank = sba("e0_rank", [P, E0])
            steps = sba("e0_steps", [P, AT])
            tiles = sba("e0_tiles", [P, NSLOT])
            lane = sba("e0_lane", [P, 1])
            below = sba("e0_below", [P, P])
            all1 = sba("e0_all1", [P, P])
            lg, ex, one, cum = (sba(f"e0_{n}", [P, AT, E0]) for n in ("shifted", "exps", "onehot", "cum"))
            total, place = sba("e0_total", [P, AT, E0]), sba("e0_place", [P, AT, E0])
            top, pos = (sba(f"e0_{n}", [P, AT]) for n in ("top", "pos"))
            cmp = sba("e0_cmp", [P, E0, AT])
            cmp2 = sba("e0_cmp2", [P, NSLOT, E0])
            ntile, ctile, base = (sba(f"e0_{n}", [P, E0]) for n in ("ntile", "ctile", "base"))
            owner = sba("e0_owner", [P, NSLOT])
            owneri = sba("e0_owneri", [P, NSLOT], I32)
            slot_rows = sba("slot_rows", [P, NSLOT, D])
            slotT = sba("slotT", [P, NSLOT * P])
            wts = Ring([sba(f"e0_wts{i}", [P, ROW]) for i in range(5)])
            hT = Ring([sba(f"e0_h{i}", [P, M0, P]) for i in range(3)])
            yrow = Ring([sba(f"e0_y{i}", [P, D]) for i in range(3)])
            wts_p = [progress(f"e0_wts{i}", 16) for i in range(5)]
            y_p = [progress(f"e0_y{i}", 16) for i in range(3)]

            pool_set(all1[:, :], 1.0)
            z_slots = pool_set(slot_rows[:, :, :], 0.0)
            ld_g = [load("e0_below", below[:, :], a["below"]),
                    load("e0_rank", rank[:, :], a["rank"].partition_broadcast(P)),
                    load("e0_steps", steps[:, :], a["steps"].partition_broadcast(P)),
                    load("e0_tiles", tiles[:, :], a["tiles"].partition_broadcast(P)),
                    load("e0_lane", lane[:, :], a["lane"])]
            slots_v = slots_in.rearrange("(j p) d -> p j d", p=P)
            wait(sp, z_slots)
            zeroed = load("slots_zero", slots_v, slot_rows[:, :, :])
            load_late_weights()

            for _ in gate_logits(1):
                pass

            def wide(v, n=AT):
                return v.unsqueeze(2).broadcast_to([P, n, E0])

            def tall(v, n=AT):
                return v.unsqueeze(1).broadcast_to([P, n, E0])

            flat = logits[:, :, :]
            wait(dve, logits_mark)
            m = dve_p.mark(dve.tensor_reduce(top[:, :], flat, AXX, ALU.max))
            wait(dve, m)
            m = dve_p.mark(dve.tensor_tensor(lg[:, :, :], flat, wide(top[:, :]), ALU.subtract))
            wait(act, m)
            ex_mark = act_p.mark(act.activation(ex[:, :, :], lg[:, :, :], ACT.Exp))
            wait(dve, m, ld_g)
            m = dve_p.mark(dve.tensor_scalar(one[:, :, :], lg[:, :, :], 0.0, None, ALU.is_equal))
            wait(dve, m)
            m = dve_p.mark(dve.tensor_tensor(one[:, :, :], one[:, :, :], tall(rank[:, :]), ALU.mult))
            wait(dve, m)
            m = dve_p.mark(dve.tensor_reduce(top[:, :], one[:, :, :], AXX, ALU.max))
            wait(dve, m)
            one_mark = dve_p.mark(dve.tensor_tensor(one[:, :, :], one[:, :, :], wide(top[:, :]), ALU.is_equal))

            onef = one[:, :, :].rearrange("p t e -> p (t e)")
            pslot, pbank = work.take()
            wait(pe, one_mark, ld_g, pslot.free)
            p_mark = pe_p.mark(pe.matmul(pbank[:, 0:TE], below[:, :], onef, start=True, stop=True))
            tslot, tbank = work.take()
            wait(pe, z_slots, tslot.free)
            m = pe_p.mark(pe.matmul(tbank[:, 0:TE], all1[:, :], onef, start=True, stop=True))
            wait(dve, m)
            total_mark = dve_p.mark(dve.tensor_copy(total[:, :, :], tbank[:, 0:TE].rearrange("p (t e) -> p t e", e=E0)))
            tslot.free = [total_mark]
            wait(dve, total_mark, z_slots)
            for e in range(E0):
                cum_mark = dve_p.mark(dve.tensor_tensor_scan(cum[:, :, e], all1[:, 0:AT], total[:, :, e], 0.0,
                                                             ALU.mult, ALU.add))
            wait(dve, cum_mark)
            m = dve_p.mark(dve.tensor_tensor(cmp[:, :, :], cum[:, AT - 1, :].unsqueeze(2).broadcast_to([P, E0, AT]),
                                             steps[:, :].unsqueeze(1).broadcast_to([P, E0, AT]), ALU.is_gt))
            wait(dve, m)
            m = dve_p.mark(dve.tensor_reduce(ntile[:, :], cmp[:, :, :], AXX, ALU.add))
            wait(dve, m)
            ct_mark = dve_p.mark(dve.tensor_tensor_scan(ctile[:, :], all1[:, 0:E0], ntile[:, :], 0.0,
                                                        ALU.mult, ALU.add))
            wait(dve, ct_mark)
            m = dve_p.mark(dve.tensor_tensor(cmp2[:, :, :], wide(tiles[:, :], NSLOT), tall(ctile[:, :], NSLOT),
                                             ALU.is_ge))
            wait(dve, m)
            m = dve_p.mark(dve.tensor_reduce(owner[:, :], cmp2[:, :, :], AXX, ALU.add))
            wait(dve, m)
            m = dve_p.mark(dve.tensor_scalar(owner[:, :], owner[:, :], float(E0 - 1), float(P), ALU.min, ALU.mult))
            wait(dve, m)
            m = dve_p.mark(dve.tensor_scalar(owner[:, :], owner[:, :], lane[:, 0:1], None, ALU.add))
            wait(dve, m)
            owner_mark = dve_p.mark(dve.tensor_copy(owneri[:, :], owner[:, :]))

            m = dve_p.mark(dve.tensor_tensor(base[:, :], ctile[:, :], ntile[:, :], ALU.subtract))
            wait(dve, m)
            m = dve_p.mark(dve.tensor_scalar(base[:, :], base[:, :], float(P), None, ALU.mult))
            wait(dve, m)
            m = dve_p.mark(dve.tensor_tensor(place[:, :, :], cum[:, :, :], total[:, :, :], ALU.subtract))
            wait(dve, m, p_mark)
            m = dve_p.mark(dve.tensor_tensor(place[:, :, :], place[:, :, :],
                                             pbank[:, 0:TE].rearrange("p (t e) -> p t e", e=E0), ALU.add))
            pslot.free = [m]
            wait(dve, m)
            m = dve_p.mark(dve.tensor_tensor(place[:, :, :], place[:, :, :], tall(base[:, :]), ALU.add))
            wait(dve, m)
            m = dve_p.mark(dve.tensor_tensor(place[:, :, :], place[:, :, :], one[:, :, :], ALU.mult))
            wait(dve, m)
            m = dve_p.mark(dve.tensor_reduce(pos[:, :], place[:, :, :], AXX, ALU.add))
            wait(dve, m)
            pos_mark = dve_p.mark(dve.tensor_copy(posi[:, :], pos[:, :]))

            wait(dve, ex_mark)
            m = dve_p.mark(dve.tensor_reduce(score[:, :], ex[:, :, :], AXX, ALU.add))
            wait(dve, m)
            score_done = dve_p.mark(dve.reciprocal(score[:, :], score[:, :]))

            def fetch_weights(j):
                slot, rows = wts.take()
                wait(pool, owner_mark, slot.free)
                return slot, rows, wts_p[j % 5].mark(pool.indirect_dma_start(
                    out=rows[:, :], out_offset=None, in_=a["e0_rows"],
                    in_offset=bass.IndirectOffsetOnAxis(ap=owneri[:, j:j + 1].bitcast(U32), axis=0)))

            scattered = progress("scattered", 16)
            wait(pool, pos_mark, zeroed)
            for t in range(AT):
                m = scattered.mark(pool.indirect_dma_start(
                    out=slots_in, out_offset=bass.IndirectOffsetOnAxis(ap=posi[:, t:t + 1].bitcast(U32),
                                                                       axis=0),
                    in_=xrows[:, t, :], in_offset=None))
            fetched = [fetch_weights(j) for j in range(3)]
            wait(sp, m)
            rows_mark = [load(f"slots{g}", slot_rows[:, g:min(g + 8, NSLOT), :], slots_v[:, g:min(g + 8, NSLOT), :])
                         for g in range(0, NSLOT, 8)]
            tbanks = Ring(bank_of[2:4])
            slotT_mark = {}
            for g in range(0, NSLOT, 4):
                n = min(4, NSLOT - g)
                slot, bank = tbanks.take()
                wait(pe, rows_mark[g // 8], slot.free)
                for t in range(n):
                    ins = pe.transpose(bank[:, t * P:(t + 1) * P], slot_rows[:, g + t, :], ident[:, :])
                m = pe_p.mark(ins)
                wait(dve, m)
                m = dve_p.mark(dve.tensor_copy(slotT[:, g * P:(g + n) * P], bank[:, 0:n * P]))
                slot.free = [m]
                for t in range(n):
                    slotT_mark[g + t] = m

            hbanks, ybanks = Ring(bank_of[4:6]), Ring(bank_of[6:8])

            def up(j):
                wslot, rows, w_mark = fetched[j]
                slot, bank = hbanks.take()
                wait(pe, w_mark, slotT_mark[j], slot.free)
                for m_ in range(M0):
                    ins = pe.matmul(bank[:, m_ * P:(m_ + 1) * P], rows[:, m_ * P:(m_ + 1) * P],
                                    slotT[:, j * P:(j + 1) * P], start=True, stop=True)
                m = pe_p.mark(ins)
                hslot, h = hT.take()
                wait(act, m, w_mark, hslot.free)
                for m_ in range(M0):
                    g = act_p.mark(act.activation(h[:, m_, :], bank[:, m_ * P:(m_ + 1) * P], ACT.Gelu,
                                                  bias=rows[:, O_B1 + m_:O_B1 + m_ + 1]))
                slot.free = [g]
                return hslot, h, g

            def down(j, hslot, h, g):
                wslot, rows, w_mark = fetched[j]
                slot, bank = ybanks.take()
                wait(pe, g, slot.free)
                for m_ in range(M0):
                    ins = pe.matmul(bank[:, 0:D], h[:, m_, :], rows[:, O_W2 + m_ * D:O_W2 + (m_ + 1) * D],
                                    start=(m_ == 0), stop=(m_ == M0 - 1))
                m = pe_p.mark(ins)
                hslot.free = [m]
                yslot, y = yrow.take()
                wait(dve, m, w_mark, yslot.free)
                r = dve_p.mark(dve.tensor_tensor(y[:, :], bank[:, 0:D], rows[:, O_B2:O_B2 + D], ALU.add))
                slot.free, wslot.free = [r], [g, m, r]
                wait(sp, r)
                stored = y_p[j % 3].mark(sp.dma_start(slots_out[j * P:(j + 1) * P, :], y[:, :]))
                yslot.free = [stored]
                return stored

            held, stored = None, {}
            for j in range(NSLOT):
                new = up(j)
                if held:
                    stored[(j - 1) % 3] = down(j - 1, *held)
                if j + 3 < NSLOT:
                    fetched.append(fetch_weights(j + 3))
                held = new
            stored[(NSLOT - 1) % 3] = down(NSLOT - 1, *held)
        barrier(*stored.values())

        def return_rows(b):
            for t in range(b * NT, (b + 1) * NT):
                wait(pool, *stored.values())
                back = progress(f"back{t}", 16).mark(pool.indirect_dma_start(
                    out=yback[:, t, :], out_offset=None, in_=slots_out,
                    in_offset=bass.IndirectOffsetOnAxis(ap=posi[:, t:t + 1].bitcast(U32), axis=0)))
                wait(dve, back, score_done, x_mark[b])
                r = dve_p.mark(dve.scalar_tensor_tensor(out=x[:, t, :], in0=yback[:, t, :], scalar=score[:, t:t + 1],
                                                        in1=x[:, t, :], op0=ALU.mult, op1=ALU.add))
            x_mark[b] = r

        def wide1(v):
            return v[:, :].unsqueeze(2).broadcast_to([P, NT, E1])

        def row1(v):
            return v[:, :].unsqueeze(1).broadcast_to([P, NT, E1])

        gate_mark = [None, None]

        def gate(b):
            yield from layer_norm_steps(b)
            yield
            g = gates[b]
            slot, bank = work.take()
            wait(pe, xnT_mark[b], ld["e1_gw"], slot.free)
            for t in range(NT):
                ins = pe.matmul(bank[:, t * E1:(t + 1) * E1], xnT[:, b, t * P:(t + 1) * P], gw[:, :],
                                start=True, stop=True)
            m = pe_p.mark(ins)
            yield
            wait(dve, m, ld["e1_gb"], ld["e1_rms"])
            m = dve_p.mark(dve.tensor_tensor(lg1[:, :, :], bank[:, 0:NT * E1].rearrange("p (t e) -> p t e", e=E1),
                                             row1(gb), ALU.add))
            slot.free = [m]
            wait(dve, m)
            m = dve_p.mark(dve.tensor_tensor(sq1[:, :, :], lg1[:, :, :], lg1[:, :, :], ALU.mult))
            wait(dve, m)
            m = dve_p.mark(dve.tensor_reduce(s1[:, :], sq1[:, :, :], AXX, ALU.add))
            wait(dve, m)
            m = dve_p.mark(dve.tensor_scalar(s1[:, :], s1[:, :], 1.0 / E1, F32_EPS, ALU.mult, ALU.add))
            yield
            wait(act, m)
            m = act_p.mark(act.activation(s1[:, :], s1[:, :], ACT.Sqrt))
            yield
            wait(dve, m)
            m = dve_p.mark(dve.reciprocal(s1[:, :], s1[:, :]))
            wait(dve, m)
            m = dve_p.mark(dve.tensor_tensor(lg1[:, :, :], lg1[:, :, :], wide1(s1), ALU.mult))
            wait(dve, m)
            m = dve_p.mark(dve.tensor_tensor(lg1[:, :, :], lg1[:, :, :], row1(rms), ALU.mult))
            wait(dve, m)
            m = dve_p.mark(dve.tensor_reduce(g[:, :], lg1[:, :, :], AXX, ALU.max))
            wait(dve, m)
            m = dve_p.mark(dve.tensor_tensor(lg1[:, :, :], lg1[:, :, :], wide1(g), ALU.subtract))
            yield
            wait(act, m)
            m = act_p.mark(act.activation(lg1[:, :, :], lg1[:, :, :], ACT.Exp, scale=2.0))
            yield
            wait(dve, m)
            m = dve_p.mark(dve.tensor_reduce(s1[:, :], lg1[:, :, :], AXX, ALU.add))
            wait(dve, m)
            m = dve_p.mark(dve.reciprocal(s1[:, :], s1[:, :]))
            wait(dve, m)
            m = dve_p.mark(dve.tensor_scalar(g[:, :], s1[:, :], GATE_EPS, None, ALU.add))
            wait(dve, m)
            m = dve_p.mark(dve.reciprocal(g[:, :], g[:, :]))
            wait(dve, m)
            gate_mark[b] = dve_p.mark(dve.tensor_tensor(g[:, :], g[:, :], s1[:, :], ALU.mult))

        u, du, zg = ([None, sb(f"{n}1", [P, KI, SEQ])] for n in ("u", "du", "zg"))
        tmp = sb("tmp", [P, SEQ])
        Y = [banks(4, 2), banks(6, 2)]
        Y_free, tmp_free = [], []
        ready = [{}, {}]

        def epilogue(b):
            nonlocal Y_free, tmp_free
            for k in range(KI):
                wait(dve, ready[b]["y"], ld["dsk"], ready[b]["z"])
                m = dve_p.mark(dve.scalar_tensor_tensor(
                    out=du[b][:, k, :], in0=u[b][:, k, :], scalar=dsk[:, k:k + 1], in1=Y[k],
                    op0=ALU.mult, op1=ALU.add))
                wait(dve, m)
                g_mark = dve_p.mark(dve.tensor_tensor(du[b][:, k, :], du[b][:, k, :], zg[b][:, k, :], ALU.mult))
            Y_free = [m]
            yield
            xs = x[:, b * NT:(b + 1) * NT, :]
            wait(dve, ld["fc2b"], x_mark[b])
            n = dve_p.mark(dve.tensor_tensor(xs, xs, fc2b[:, :].unsqueeze(1).broadcast_to([P, NT, D]), ALU.add))
            for c in range(NC):
                slot, bank = work.take()
                cs = slice(c * CH, (c + 1) * CH)
                wait(pe, g_mark, ld["outp"], slot.free)
                for k in range(KI):
                    ins = pe.matmul(bank, outp[:, k, :], du[b][:, k, cs], start=(k == 0), stop=(k == KI - 1))
                m = pe_p.mark(ins)
                wait(act, m, tmp_free)
                m = act_p.mark(act.copy(tmp[:, cs], bank))
                slot.free = [m]
                yield
                slot, bank = work.take()
                wait(pe, m, ld["fc2"], slot.free)
                for t in range(4):
                    tt = 4 * c + t
                    ins = pe.matmul(bank[:, t * P:(t + 1) * P], tmp[:, tt * P:(tt + 1) * P], fc2[:, :],
                                    start=True, stop=True)
                m = pe_p.mark(ins)
                yield
                xs = x[:, b * NT + 4 * c:b * NT + 4 * c + 4, :]
                wait(dve, m, n)
                x_mark[b] = dve_p.mark(dve.tensor_tensor(xs, tile_bank(bank), xs, ALU.add))
                slot.free = [x_mark[b]]
                yield
            tmp_free = [m]

        with ExitStack() as scope:
            def sba(name, shape, dt=F32):
                return sb(name, shape, dt, scope)

            PAD = DCONV - 1
            h1T = sba("h1T", [P, SEQ])
            xc = sba("xc", [P, KI, PAD + SEQ])
            xd = sba("xd", [P, SEQ])
            for n, t in (("u", u), ("du", du), ("zg", zg)):
                t[0] = sba(f"{n}0", [P, KI, SEQ])
            dt = [sba(f"dt{b}", [P, KI, SEQ]) for b in range(B)]
            xdr = [sba(f"xdr{b}", [P, SEQ], F32R) for b in range(B)]
            dA, dBu, hs, hc, cc = (Ring([sba(f"{n}{i}", [P, SEQ]) for i in range(k)]) for n, k in
                                       (("dA", 3), ("dBu", 3), ("hs", 3), ("hc", 3), ("cc", 2)))
            Brow = banks(2, 2)
            Brow_free = []
            Crow = Ring(bank_of[1:2])

            z = pool_set(xc[:, :, 0:PAD], 0.0)
            wait(dve, ld["pick"])
            pick_mark = dve_p.mark(dve.tensor_copy(pickr[:, :], pick[:, :]))
            wait(act, ld["alog"])
            A_mark = act_p.mark(act.activation(alog[:, :, :], alog[:, :, :], ACT.Exp))
            wait(dve, A_mark)
            A_mark = dve_p.mark(dve.tensor_scalar(alog[:, :, :], alog[:, :, :], -1.0, None, ALU.mult))
            h1T_free, xc_free, xd_free = [], [], []

            def prologue(b):
                nonlocal h1T_free, xc_free, xd_free, tmp_free
                yield from layer_norm_steps(b)
                yield
                for c in range(NC):
                    slot, bank = work.take()
                    wait(pe, xnT_mark[b], ld["fc1"], slot.free)
                    m = pe_p.mark(pe.matmul(bank, fc1[:, :], xnT[:, b, c * CH:(c + 1) * CH], start=True, stop=True))
                    wait(act, m, ld["fc1b"], h1T_free)
                    h_mark = act_p.mark(act.activation(h1T[:, c * CH:(c + 1) * CH], bank, ACT.Identity,
                                                       bias=fc1b[:, 0:1]))
                    slot.free = [h_mark]
                xnT_free[b] = [m]
                yield
                conv = [None] * KI
                for k in range(2 * KI):
                    for c in range(NC):
                        slot, bank = work.take()
                        wait(pe, h_mark, ld["inp"], slot.free)
                        m = pe_p.mark(pe.matmul(bank, inp[:, k * P:(k + 1) * P], h1T[:, c * CH:(c + 1) * CH],
                                                start=True, stop=True))
                        if k < KI:
                            wait(act, m, xc_free)
                            n = act_p.mark(act.copy(xc[:, k, PAD + c * CH:PAD + (c + 1) * CH], bank))
                        else:
                            wait(act, m)
                            n = act_p.mark(act.activation(zg[b][:, k - KI, c * CH:(c + 1) * CH], bank, ACT.Silu))
                            ready[b]["z"] = n
                        slot.free = [n]
                    yield
                    if k < KI:
                        ub = u[b][:, k, :]
                        wait(dve, n, z, ld["cw"], ld["cb"])
                        v = dve_p.mark(dve.tensor_scalar(ub, xc[:, k, 0:SEQ], cw[:, k, 0:1], cb[:, k:k + 1],
                                                         ALU.mult, ALU.add))
                        for w in range(1, DCONV):
                            wait(dve, v)
                            v = dve_p.mark(dve.scalar_tensor_tensor(
                                out=ub, in0=xc[:, k, w:w + SEQ], scalar=cw[:, k, w:w + 1], in1=ub,
                                op0=ALU.mult, op1=ALU.add))
                        conv[k] = v
                        yield
                h1T_free, xc_free = [m], conv
                for k in range(KI):
                    wait(act, conv[k])
                    u_mark = act_p.mark(act.activation(u[b][:, k, :], u[b][:, k, :], ACT.Silu))
                yield
                for c in range(NC):
                    slot, bank = work.take()
                    cs = slice(c * CH, (c + 1) * CH)
                    wait(pe, u_mark, ld["xpj"], slot.free)
                    for k in range(KI):
                        ins = pe.matmul(bank, xpj[:, k, :], u[b][:, k, cs], start=(k == 0), stop=(k == KI - 1))
                    m = pe_p.mark(ins)
                    wait(act, m, xd_free)
                    act_p.mark(act.copy(xdr[b][:, cs], bank))
                    xd_mark = act_p.mark(act.copy(xd[:, cs], bank))
                    slot.free = [xd_mark]
                yield
                wait(dve, xd_mark)
                ready[b]["xdr"] = dve_p.mark(dve.tensor_tensor(xdr[b][LO:P, :], xd[LO:P, :], xdr[b][LO:P, :],
                                                               ALU.subtract))
                yield
                for k in range(KI):
                    for c in range(NC):
                        slot, bank = work.take()
                        cs = slice(c * CH, (c + 1) * CH)
                        wait(pe, xd_mark, ld["dtp"], slot.free)
                        m = pe_p.mark(pe.matmul(bank, dtp[:, k * P:(k + 1) * P], xd[:, cs], start=True, stop=True))
                        wait(act, m, ld["dtb"])
                        n = act_p.mark(act.activation(dt[b][:, k, cs], bank, ACT.Identity, bias=dtb[:, k:k + 1]))
                        slot.free = [n]
                xd_free = [m, ready[b]["xdr"]]
                yield
                softs = (tmp, h1T)
                for k in range(KI):
                    wait(act, n, tmp_free, h1T_free)
                    m = act_p.mark(act.activation(softs[k][:, :], dt[b][:, k, :], ACT.Abs))
                    wait(act, m)
                    m = act_p.mark(act.activation(softs[k][:, :], softs[k][:, :], ACT.Exp, scale=-1.0))
                yield
                logs = []
                for k in range(KI):
                    wait(act, m)
                    logs.append(act_p.mark(act.activation(softs[k][:, :], softs[k][:, :], ACT.Ln, bias=1.0)))
                yield
                for k in range(KI):
                    wait(dve, logs[k])
                    m = dve_p.mark(dve.scalar_tensor_tensor(
                        out=dt[b][:, k, :], in0=dt[b][:, k, :], scalar=0.0, in1=softs[k][:, :], op0=ALU.max, op1=ALU.add))
                    ready[b]["dt", k] = m
                    wait(dve, m, u_mark)
                    ready[b]["du", k] = dve_p.mark(dve.tensor_tensor(du[b][:, k, :], dt[b][:, k, :], u[b][:, k, :],
                                                                     ALU.mult))
                tmp_free, h1T_free = [m], [m]
                yield

            def recurrence(b):
                nonlocal Brow_free

                def spread(row, bank, c):
                    wait(pe, ready[b]["xdr"], pick_mark)
                    return pe_p.mark(pe.matmul(bank, pickr[:, row:row + 1].broadcast_to([P, P]),
                                               xdr[b][:, c * CH:(c + 1) * CH], start=True, stop=True))

                def spread_B(n):
                    wait(pe, Brow_free)
                    return [spread(n, Brow[:, c * CH:(c + 1) * CH], c) for c in range(NC)]

                def spread_C(n, c, row):
                    tslot, tile = row
                    slot, bank = Crow.take()
                    wait(pe, slot.free)
                    m = spread(NS + n, bank, c)
                    wait(act, m, tslot.free)
                    slot.free = [act_p.mark(act.copy(tile[:, c * CH:(c + 1) * CH], bank))]
                    return slot.free

                def decays(k, n):
                    slot, decay = dA.take()
                    wait(act, ready[b]["dt", k], A_mark, slot.free)
                    return slot, decay, act_p.mark(act.activation(decay[:, :], dt[b][:, k, :], ACT.Exp,
                                                                  scale=alog[:, k, n:n + 1]))

                def add_state(k, n, slot, product, o_mark):
                    wait(pe, o_mark, Y_free)
                    for c in range(NC):
                        ins = pe.matmul(Y[k][:, c * CH:(c + 1) * CH], ident[:, :], product[:, c * CH:(c + 1) * CH],
                                        start=(n == 0), stop=(n == NS - 1))
                    ready[b]["y"] = pe_p.mark(ins)
                    slot.free = [ready[b]["y"]]

                b_mark, C_next = spread_B(0), cc.take()
                for c in range(NC):
                    c_next = spread_C(0, c, C_next)
                order = [(n, k) for n in range(NS) for k in range(KI)]
                decay_of = {o: decays(o[1], o[0]) for o in order[:2]}
                waiting = []
                for n in range(NS):
                    gains = []
                    for k in range(KI):
                        gslot, gain = dBu.take()
                        wait(dve, b_mark, ready[b]["du", k], gslot.free)
                        g_mark = dve_p.mark(dve.tensor_tensor(gain[:, :], Brow, du[b][:, k, :], ALU.mult))
                        gains.append((gslot, gain, g_mark))
                    Brow_free = [g_mark]
                    (cslot, crow), c_mark = C_next, c_next
                    cslot.free = []
                    if n + 1 < NS:
                        C_next = cc.take()
                    for k in range(KI):
                        at = n * KI + k
                        if n + 1 < NS:
                            c_next = spread_C(n + 1, k, C_next)
                            if k == KI - 1:
                                b_mark = spread_B(n + 1)
                        if at + 2 < len(order):
                            decay_of[order[at + 2]] = decays(order[at + 2][1], order[at + 2][0])
                        aslot, decay, a_mark = decay_of.pop((n, k))
                        gslot, gain, g_mark = gains[k]
                        sslot, state = hs.take()
                        wait(dve, g_mark, a_mark, sslot.free)
                        s_mark = dve_p.mark(dve.tensor_tensor_scan(state[:, :], decay[:, :], gain[:, :], 0.0,
                                                                   ALU.mult, ALU.add))
                        aslot.free, gslot.free = [s_mark], [s_mark]
                        oslot, product = hc.take()
                        wait(pool, s_mark, c_mark, oslot.free)
                        pool_alone()
                        o_mark = pool_p.mark(pool.tensor_tensor(product[:, :], state[:, :], crow[:, :], ALU.mult))
                        sslot.free = [o_mark]
                        cslot.free.append(o_mark)
                        waiting.append((k, n, oslot, product, o_mark))
                        if len(waiting) > 2:
                            add_state(*waiting.pop(0))
                        yield
                for w in waiting:
                    add_state(*w)

            return_rows(0)
            first = prologue(0)
            next(first)
            return_rows(1)
            for _ in first:
                pass
            work = Ring(bank_of[0:1])
            interleave(recurrence(0), prologue(1), 0.5)
            interleave(recurrence(1), chain(epilogue(0), gate(0)), 0.8)
        barrier()

        with ExitStack() as scope:
            def sba(name, shape, dt=F32):
                return sb(name, shape, dt, scope)

            def pair_of(name, shape):
                return [sba(f"{name}_{n}", shape, F32R) for n in ("hi", "lo")]

            w1s, w2s = pair_of("e1_w1", [P, E1, F1]), pair_of("e1_w2", [P, M1, D])
            xs_ = [pair_of(f"e1_x{b}", [P, SEQ]) for b in range(B)]
            b2s = sba("e1_b2s", [P, 1])
            hf = Ring([sba(f"e1_h{i}", [P, CH]) for i in range(4)])
            hr = Ring([pair_of(f"e1_hr{i}", [P, CH]) for i in range(4)])
            yT = Ring([sba(f"e1_yT{i}", [P, CH]) for i in range(2)])
            hid, ysum = Ring(bank_of[2:6]), Ring(bank_of[6:8])
            turned = Ring(bank_of[1:2])

            def split(parts, src, hi_on=dve_p, lo_on=dve_p):
                engine = {dve_p: dve, act_p: act, pool_p: pool}
                copy = engine[hi_on].copy if hi_on is act_p else engine[hi_on].tensor_copy
                hi = hi_on.mark(copy(parts[0], src))
                wait(engine[lo_on], hi)
                if lo_on is pool_p:
                    pool_alone()
                return lo_on.mark(engine[lo_on].tensor_tensor(parts[1], src, parts[0], ALU.subtract))

            xs_mark, w1_mark, w2_mark = {}, {}, {}

            def split_input(b):
                for c in range(NC):
                    cs = slice(c * CH, (c + 1) * CH)
                    wait(act, xnT_mark[b])
                    wait(dve, xnT_mark[b])
                    xs_mark[b, c] = split([p[:, cs] for p in xs_[b]], xnT[:, b, cs], act_p, dve_p)
                    yield

            def split_w1(e):
                wait(act, ld["e1_w1"])
                wait(pool, ld["e1_w1"])
                w1_mark[e] = split([w[:, e, :] for w in w1s], ew1[:, e, :], act_p, pool_p)

            def split_w2(e):
                ms = slice(e * F1 // P, (e + 1) * F1 // P)
                wait(act, ld["e1_w2"])
                wait(pool, ld["e1_w2"])
                w2_mark[e] = split([w[:, ms, :] for w in w2s], ew2[:, ms, :], act_p, pool_p)

            def second_input():
                yield from epilogue(1)
                yield from gate(1)
                yield from split_input(1)

            split_w1(0)
            for _ in split_input(0):
                pass
            split_w2(0)
            side = second_input()
            next(side)
            for bank in bank_of[4:8]:
                bank.free = Y_free
            wait(dve, ld["e1_b2"])
            b2_mark = dve_p.mark(dve.tensor_reduce(b2s[:, :], eb2[:, :], AXX, ALU.add))
            HI_LO = ((0, 0), (0, 1), (1, 0))

            def up(b, c, m_):
                e, f = divmod(m_, F1 // P)
                slot, bank = hid.take()
                wait(pe, w1_mark[e], xs_mark[b, c], slot.free)
                for n, (i, j) in enumerate(HI_LO):
                    ins = pe.matmul(bank, w1s[i][:, e, f * P:(f + 1) * P], xs_[b][j][:, c * CH:(c + 1) * CH],
                                    start=(n == 0), stop=(n == 2))
                m = pe_p.mark(ins)
                fslot, h = hf.take()
                wait(act, m, ld["e1_b1"], fslot.free)
                g = act_p.mark(act.activation(h[:, :], bank, ACT.Gelu, bias=eb1[:, m_:m_ + 1]))
                slot.free = [g]
                rslot, parts = hr.take()
                wait(dve, g, rslot.free)
                r = split([p[:, :] for p in parts], h[:, :])
                fslot.free = [r]
                return rslot, parts, r

            def down(m_, bank, rslot, parts, r):
                wait(pe, r, w2_mark[m_ * P // F1])
                for n, (i, j) in enumerate(HI_LO):
                    ins = pe.matmul(bank, w2s[i][:, m_, :], parts[j][:, :], start=(m_ == 0 and n == 0),
                                    stop=(m_ == M1 - 1 and n == 2))
                m = pe_p.mark(ins)
                rslot.free = [m]
                return m

            def finish(b, c, slot, bank, m):
                yslot, y = yT.take()
                wait(act, m, b2_mark, yslot.free)
                m = act_p.mark(act.activation(y[:, :], bank, ACT.Identity, bias=b2s[:, 0:1]))
                slot.free = [m]
                slot, bank = turned.take()
                wait(pe, m, slot.free)
                for t in range(4):
                    ins = pe.transpose(bank[:, t * P:(t + 1) * P], y[:, t * P:(t + 1) * P], ident[:, :])
                m = pe_p.mark(ins)
                yslot.free = [m]
                wait(dve, m, gate_mark[b])
                for t in range(4):
                    tt = 4 * c + t
                    xs = x[:, b * NT + tt, :]
                    r = dve_p.mark(dve.scalar_tensor_tensor(out=xs, in0=bank[:, t * P:(t + 1) * P],
                                                            scalar=gates[b][:, tt:tt + 1], in1=xs,
                                                            op0=ALU.mult, op1=ALU.add))
                slot.free = [r]
                wait(sp, r)
                at = slice(b * NT + 4 * c, b * NT + 4 * c + 4)
                return progress(f"store{b}{c}", 16).mark(sp.dma_start(out_d[:, at, :], x[:, at, :]))

            LAG = 3
            units = [(b, c, m_) for b in range(B) for c in range(NC) for m_ in range(M1)]
            ups, stores, sums = {}, [], {}
            for n in range(len(units) + LAG):
                if n < len(units):
                    b, c, m_ = units[n]
                    if n >= LAG:
                        next(side, None)
                    if n < M1 and m_ % (F1 // P) == 0 and m_ // (F1 // P) + 1 < E1:
                        split_w1(m_ // (F1 // P) + 1)
                        split_w2(m_ // (F1 // P) + 1)
                    if b == 1:
                        for _ in side:
                            pass
                    ups[n] = up(b, c, m_)
                if n >= LAG:
                    b, c, m_ = units[n - LAG]
                    if m_ == 0:
                        sums[b, c] = ysum.take()
                        wait(pe, sums[b, c][0].free)
                    m = down(m_, sums[b, c][1], *ups.pop(n - LAG))
                    if m_ == M1 - 1:
                        stores.append(finish(b, c, *sums[b, c], m))
            wait(sp, stores)



def _layout(i):
    f = {k: np.asarray(v) for k, v in i.items()}
    A, G, S, M = "L0_attn_", "L0_ffn_", "L1_attn_", "L1_ffn_"
    heads = lambda w: w.transpose(2, 0, 1).reshape(D, H * DH)
    cols = lambda v, k: v.reshape(k, P).T
    o = {
        "x": f[A + "x"].reshape(B * SEQ, D),
        "ident": np.eye(P, dtype=np.float32),
        "wq": heads(f[A + "W_Q"]), "wk": heads(f[A + "W_K"]), "wv": heads(f[A + "W_V"]),
        "bq": cols(f[A + "b_Q"], NPAIR), "bk": cols(f[A + "b_K"], NPAIR),
        "bv": f[A + "b_V"].reshape(H * DH),
        "wo": f[A + "W_O"].transpose(0, 2, 1).reshape(NPAIR, P, D).transpose(1, 0, 2).reshape(P, NPAIR * D),
        "bo": f[A + "b_O"],
        "rank": np.arange(E0, 0, -1, dtype=np.float32),
        "steps": np.arange(B * NT, dtype=np.float32) * P, "tiles": np.arange(B * NT + E0 - 1, dtype=np.float32),
        "lane": np.arange(P, dtype=np.float32).reshape(P, 1), "below": np.triu(np.ones((P, P), np.float32), 1),
        "e0_wg": f[G + "wg"],
        "e0_rows": np.concatenate([
            f[G + "w1"].reshape(E0 * P, F0), f[G + "b1"].reshape(E0, M0, P).transpose(0, 2, 1).reshape(E0 * P, M0),
            f[G + "w2"].reshape(E0, M0, P, D).transpose(0, 2, 1, 3).reshape(E0 * P, M0 * D),
            np.repeat(f[G + "b2"], P, axis=0)], axis=1),
        "fc1": f[S + "fc1_w"].T, "fc1b": f[S + "fc1_b"].reshape(P, 1), "inp": f[S + "in_proj_w"].T,
        "cw": f[S + "conv_w"].reshape(KI, P, DCONV).transpose(1, 0, 2), "cb": cols(f[S + "conv_b"], KI),
        "dtb": cols(f[S + "dt_proj_b"], KI),
        "alog": f[S + "A_log"].reshape(KI, P, NS).transpose(1, 0, 2), "dsk": cols(f[S + "D"], KI),
        "outp": f[S + "out_proj_w"].T.reshape(KI, P, D).transpose(1, 0, 2),
        "fc2": f[S + "fc2_w"].T, "fc2b": f[S + "fc2_b"],
        "e1_gw": f[M + "gate_w"].T, "e1_gb": f[M + "gate_b"], "e1_rms": f[M + "rms_w"],
        "e1_w1": f[M + "w1"], "e1_b1": cols(f[M + "b1"], M1), "e1_w2": f[M + "w2"], "e1_b2": f[M + "b2"].T,
    }
    wred = np.zeros((P, P), np.float32)
    wred[:, :GATE] = f[G + "wg_red"].T
    o["e0_wred"] = wred
    rows = DTR + 2 * NS
    xpj = np.zeros((P, KI, P), np.float32)
    xw = f[S + "x_proj_w"].T.reshape(KI, P, rows).transpose(1, 0, 2)
    xpj[:, :, :rows] = xw
    xpj[:, :, LO:LO + rows] = xw
    o["xpj"] = xpj
    dtp = np.zeros((P, DI), np.float32)
    dtp[:DTR] = f[S + "dt_proj_w"].T
    o["dtp"] = dtp
    pick = np.zeros((P, 2 * NS), np.float32)
    for n in range(2 * NS):
        pick[DTR + n, n] = pick[LO + DTR + n, n] = 1.0
    o["pick"] = pick
    return {k: np.ascontiguousarray(v) for k, v in o.items()}


def kernel(**inputs):
    from concourse import bacc
    from concourse.bass_utils import run_bass_kernel_spmd

    arrays = _layout(inputs)
    nc = bacc.Bacc("TRN2", target_bir_lowering=False, num_devices=1)
    ins = {k: nc.dram_tensor("in_" + k, v.shape, mybir.dt.from_np(v.dtype), kind="ExternalInput").ap()
           for k, v in arrays.items()}
    out = nc.dram_tensor("out_x", (B * SEQ, D), F32, kind="ExternalOutput").ap()
    two_layer_program(nc, ins, out)
    r = run_bass_kernel_spmd(nc, [{"in_" + k: v for k, v in arrays.items()}], core_ids=[0])
    return r.results[0]["out_x"].reshape(B, SEQ, D)
```
